# Optimizing a Trainium2 kernel written in Bass

```python
import numpy as np
import jax
import jax.numpy as jnp

def _softmax(x, axis=-1):
    return jax.nn.softmax(x, axis=axis)

def _gelu(x):
    return jax.nn.gelu(x, approximate=True)

def _silu(x):
    return jax.nn.silu(x)

def _sigmoid(x):
    return jax.nn.sigmoid(x)

def _layernorm(x, axis=-1, eps=1e-05):
    m = jnp.mean(x, axis=axis, keepdims=True)
    v = jnp.var(x, axis=axis, keepdims=True)
    return (x - m) / jnp.sqrt(v + eps)

def _scatter_add(tgt, idx, src, axis=0):
    return tgt.at[idx].add(src)

def _segment_sum(src, seg, n):
    return jax.ops.segment_sum(src, seg, n)
kernel_name = 'mk_gnn_preln_d4_gnn_r32_2cb539'

def setup_inputs(seed: int=0):
    np.random.seed(seed)
    _w = jnp.asarray

    def _rec_inputs():
        import jax
        import jax.numpy as jnp
        _gk = jax.random.key(seed)
        x = -0.0003713 + 1 * jax.random.normal(jax.random.fold_in(_gk, 1), (3125, 128), jnp.float32)
        src = jax.random.randint(jax.random.fold_in(_gk, 2), (50000,), 0, 3125, jnp.int32)
        dst = jax.random.randint(jax.random.fold_in(_gk, 3), (50000,), 0, 3125, jnp.int32)
        _o = jnp.argsort(dst, stable=True)
        src = src[_o]
        dst = dst[_o]
        edge_weight = jax.random.uniform(jax.random.fold_in(_gk, 13), (50000,), jnp.float32, 0.0, 1)
        return (x, src, dst, edge_weight)
    x, src, dst, edge_weight = _rec_inputs()

    def _L0_gnn_setup():
        import jax, jax.numpy as jnp
        import numpy as np
        N_NODES = 3125
        N_EDGES = 50000
        DIM_IN = 128
        DIM_OUT = 128
        key = jax.random.key(seed)
        k1, k2, k3, k4, k5, k6 = jax.random.split(key, 6)
        stdv = 1.0 / np.sqrt(DIM_OUT)
        inputs = {'input': jax.random.normal(k1, (N_NODES, DIM_IN), dtype=jnp.float32), 'edge_src': jax.random.randint(k2, (N_EDGES,), 0, N_NODES, dtype=jnp.int32), 'edge_dst': jax.random.randint(k3, (N_EDGES,), 0, N_NODES, dtype=jnp.int32), 'edge_weight': jax.random.uniform(k4, (N_EDGES,), dtype=jnp.float32), 'weight': jax.random.uniform(k5, (DIM_IN, DIM_OUT), dtype=jnp.float32, minval=-stdv, maxval=stdv), 'bias': jax.random.uniform(k6, (DIM_OUT,), dtype=jnp.float32, minval=-stdv, maxval=stdv)}
        return inputs
    _L0_gnn_all = _L0_gnn_setup()
    _L0_gnn_in = {k: v for k, v in _L0_gnn_all.items() if k in ('weight', 'bias')}
    del _L0_gnn_all

    def _L1_gnn_setup():
        import jax, jax.numpy as jnp
        import numpy as np
        N = 3125
        E = 25000
        D = 128
        OUT = 128
        key = jax.random.key(seed)
        k = jax.random.split(key, 6)
        x = jax.random.normal(k[0], (N, D), dtype=jnp.float32)
        edge_index = jax.random.randint(k[1], (2, E), 0, N, dtype=jnp.int64)
        Wl = jax.random.normal(k[2], (D, OUT), dtype=jnp.float32) / np.sqrt(D)
        bl = jax.random.normal(k[3], (OUT,), dtype=jnp.float32) * 0.01
        Wr = jax.random.normal(k[4], (D, OUT), dtype=jnp.float32) / np.sqrt(D)
        br = jax.random.normal(k[5], (OUT,), dtype=jnp.float32) * 0.01
        return {'x': x, 'edge_index': edge_index, 'Wl': Wl, 'bl': bl, 'Wr': Wr, 'br': br}
    _L1_gnn_all = _L1_gnn_setup()
    _L1_gnn_in = {k: v for k, v in _L1_gnn_all.items() if k in ('Wl', 'bl', 'Wr', 'br')}
    del _L1_gnn_all

    def _L2_gnn_setup():
        import jax, jax.numpy as jnp
        import numpy as np
        N, E, D, H, LAYERS = (50000, 25000, 128, 8, 2)
        LRELU_ALPHA = 0.2

        def _seg_softmax(logits, seg, n):
            m = jax.ops.segment_max(logits, seg, num_segments=n)
            z = jnp.exp(logits - m[seg])
            s = jax.ops.segment_sum(z, seg, num_segments=n)
            return z / jnp.maximum(s[seg], 1e-16)

        def _gat_layer(x, src, dst, W, a_src, a_dst, concat):
            n = x.shape[0]
            outs = []
            for h in range(W.shape[0]):
                Wh = x @ W[h]
                es = Wh @ a_src[h]
                ed = Wh @ a_dst[h]
                e = jax.nn.leaky_relu(es[src] + ed[dst], LRELU_ALPHA)
                att = _seg_softmax(e, dst, n)
                out = jax.ops.segment_sum(att[:, None] * Wh[src], dst, num_segments=n)
                outs.append(out)
            if concat:
                return jax.nn.elu(jnp.concatenate(outs, axis=-1))
            return jnp.mean(jnp.stack(outs, axis=0), axis=0)

        def _rel_gcn_layer(x, src, dst, w, W):
            n = x.shape[0]
            deg = jax.ops.segment_sum(w, dst, num_segments=n)
            norm = w / jnp.maximum(deg[dst], 1e-16)
            h = x @ W
            agg = jax.ops.segment_sum(norm[:, None] * h[src], dst, num_segments=n)
            return jax.nn.relu(agg)
        key = jax.random.key(seed)
        ks = jax.random.split(key, 12)
        s = 1.0 / np.sqrt(D)
        return {'x': jax.random.normal(ks[0], (N, D), dtype=jnp.float32), 'edge_index': jax.random.randint(ks[1], (2, E), 0, N, dtype=jnp.int64), 'edge_weight': jax.random.uniform(ks[2], (E,), dtype=jnp.float32), 'gat_W0': jax.random.normal(ks[3], (H, D, D // H), dtype=jnp.float32) * s, 'gat_a0_src': jax.random.normal(ks[4], (H, D // H), dtype=jnp.float32) * s, 'gat_a0_dst': jax.random.normal(ks[5], (H, D // H), dtype=jnp.float32) * s, 'gat_W1': jax.random.normal(ks[6], (H, D, D), dtype=jnp.float32) * s, 'gat_a1_src': jax.random.normal(ks[7], (H, D), dtype=jnp.float32) * s, 'gat_a1_dst': jax.random.normal(ks[8], (H, D), dtype=jnp.float32) * s, 'gcn_W0': jax.random.normal(ks[9], (D, D), dtype=jnp.float32) * s, 'gcn_W1': jax.random.normal(ks[10], (D, D), dtype=jnp.float32) * s}
    _L2_gnn_all = _L2_gnn_setup()
    _L2_gnn_in = {k: v for k, v in _L2_gnn_all.items() if k in ('gat_W0', 'gat_a0_src', 'gat_a0_dst', 'gat_W1', 'gat_a1_src', 'gat_a1_dst', 'gcn_W0', 'gcn_W1')}
    del _L2_gnn_all

    def _L3_gnn_setup():
        import jax, jax.numpy as jnp
        import numpy as np
        STEP = 10

        def _diffusion(x, edge_index, t):
            N = x.shape[0]
            self_loop = jnp.arange(N, dtype=edge_index.dtype)
            row = jnp.concatenate([edge_index[0], self_loop])
            col = jnp.concatenate([edge_index[1], self_loop])
            deg = jax.ops.segment_sum(jnp.ones_like(col, x.dtype), col, num_segments=N)
            dinv = deg ** (-0.5)
            norm = dinv[row] * dinv[col]
            t_norm = jax.nn.softmax(t, axis=0)

            def step(h, _):
                h = jax.ops.segment_sum(norm[:, None] * h[row], col, num_segments=N)
                return (h, h)
            _, hs = jax.lax.scan(step, x, None, length=STEP - 1)
            return t_norm[0] * x + jnp.einsum('kf,knf->nf', t_norm[1:], hs)
        key = jax.random.key(seed)
        k1, k2, k3, k4, k5 = jax.random.split(key, 5)
        N, E, F_in, F_out, K = (50000, 18750, 128, 128, 1)
        x = jax.random.normal(k1, (N, F_in), dtype=jnp.float32)
        edge_index = jax.random.randint(k2, (2, E), 0, N, dtype=jnp.int64)
        t = jax.random.normal(k3, (STEP, F_in), dtype=jnp.float32) * 0.1
        glorot = lambda k, shape: jax.random.uniform(k, shape, jnp.float32, -1.0, 1.0) * jnp.sqrt(6.0 / (shape[-2] + shape[-1]))
        init_weight = glorot(k4, (K, F_in, F_out))
        root_weight = glorot(k5, (1, K, F_in, F_out))
        bias = jnp.zeros((1, K, 1, F_out), dtype=jnp.float32)
        return {'x': x, 'edge_index': edge_index, 't': t, 'init_weight': init_weight, 'root_weight': root_weight, 'bias': bias}
    _L3_gnn_all = _L3_gnn_setup()
    _L3_gnn_in = {k: v for k, v in _L3_gnn_all.items() if k in ('t', 'init_weight', 'root_weight', 'bias')}
    del _L3_gnn_all
    return {'x': x, 'src': src, 'dst': dst, 'edge_weight': edge_weight, 'L0_gnn_weight': _L0_gnn_in['weight'], 'L0_gnn_bias': _L0_gnn_in['bias'], 'L1_gnn_Wl': _L1_gnn_in['Wl'], 'L1_gnn_bl': _L1_gnn_in['bl'], 'L1_gnn_Wr': _L1_gnn_in['Wr'], 'L1_gnn_br': _L1_gnn_in['br'], 'L2_gnn_gat_W0': _L2_gnn_in['gat_W0'], 'L2_gnn_gat_a0_src': _L2_gnn_in['gat_a0_src'], 'L2_gnn_gat_a0_dst': _L2_gnn_in['gat_a0_dst'], 'L2_gnn_gat_W1': _L2_gnn_in['gat_W1'], 'L2_gnn_gat_a1_src': _L2_gnn_in['gat_a1_src'], 'L2_gnn_gat_a1_dst': _L2_gnn_in['gat_a1_dst'], 'L2_gnn_gcn_W0': _L2_gnn_in['gcn_W0'], 'L2_gnn_gcn_W1': _L2_gnn_in['gcn_W1'], 'L3_gnn_t': _L3_gnn_in['t'], 'L3_gnn_init_weight': _L3_gnn_in['init_weight'], 'L3_gnn_root_weight': _L3_gnn_in['root_weight'], 'L3_gnn_bias': _L3_gnn_in['bias']}

def reference(x, src, dst, edge_weight, L0_gnn_weight, L0_gnn_bias, L1_gnn_Wl, L1_gnn_bl, L1_gnn_Wr, L1_gnn_br, L2_gnn_gat_W0, L2_gnn_gat_a0_src, L2_gnn_gat_a0_dst, L2_gnn_gat_W1, L2_gnn_gat_a1_src, L2_gnn_gat_a1_dst, L2_gnn_gcn_W0, L2_gnn_gcn_W1, L3_gnn_t, L3_gnn_init_weight, L3_gnn_root_weight, L3_gnn_bias):
    import jax
    import jax.numpy as jnp

    def _L0_gnn_ref(input, edge_src, edge_dst, edge_weight, weight, bias):
        import jax, jax.numpy as jnp
        import numpy as np
        N_NODES = 3125
        N_EDGES = 50000
        DIM_IN = 128
        DIM_OUT = 128
        support = jnp.matmul(input, weight)
        gathered = support[edge_src] * edge_weight[:, None]
        output = jax.ops.segment_sum(gathered, edge_dst, num_segments=input.shape[0])
        return output + bias

    def _L1_gnn_ref(x, edge_index, Wl, bl, Wr, br):
        import jax, jax.numpy as jnp
        import numpy as np
        N = 3125
        E = 25000
        D = 128
        OUT = 128
        n = x.shape[0]
        tgt = edge_index[0]
        nbr = edge_index[1]
        agg_sum = jax.ops.segment_sum(x[nbr], tgt, num_segments=n)
        deg = jax.ops.segment_sum(jnp.ones((edge_index.shape[1],), x.dtype), tgt, num_segments=n)
        agg = agg_sum / jnp.maximum(deg, 1.0)[:, None]
        out = jax.nn.relu(x @ Wl + bl + agg @ Wr + br)
        norm = jnp.linalg.norm(out, axis=1, keepdims=True) + 1e-06
        return out / norm

    def _L2_gnn_ref(x, edge_index, edge_weight, gat_W0, gat_a0_src, gat_a0_dst, gat_W1, gat_a1_src, gat_a1_dst, gcn_W0, gcn_W1):
        import jax, jax.numpy as jnp
        import numpy as np
        N, E, D, H, LAYERS = (50000, 25000, 128, 8, 2)
        LRELU_ALPHA = 0.2

        def _seg_softmax(logits, seg, n):
            m = jax.ops.segment_max(logits, seg, num_segments=n)
            z = jnp.exp(logits - m[seg])
            s = jax.ops.segment_sum(z, seg, num_segments=n)
            return z / jnp.maximum(s[seg], 1e-16)

        def _gat_layer(x, src, dst, W, a_src, a_dst, concat):
            n = x.shape[0]
            outs = []
            for h in range(W.shape[0]):
                Wh = x @ W[h]
                es = Wh @ a_src[h]
                ed = Wh @ a_dst[h]
                e = jax.nn.leaky_relu(es[src] + ed[dst], LRELU_ALPHA)
                att = _seg_softmax(e, dst, n)
                out = jax.ops.segment_sum(att[:, None] * Wh[src], dst, num_segments=n)
                outs.append(out)
            if concat:
                return jax.nn.elu(jnp.concatenate(outs, axis=-1))
            return jnp.mean(jnp.stack(outs, axis=0), axis=0)

        def _rel_gcn_layer(x, src, dst, w, W):
            n = x.shape[0]
            deg = jax.ops.segment_sum(w, dst, num_segments=n)
            norm = w / jnp.maximum(deg[dst], 1e-16)
            h = x @ W
            agg = jax.ops.segment_sum(norm[:, None] * h[src], dst, num_segments=n)
            return jax.nn.relu(agg)
        src, dst = (edge_index[0], edge_index[1])
        gat_params = [(gat_W0, gat_a0_src, gat_a0_dst), (gat_W1, gat_a1_src, gat_a1_dst)]
        gcn_params = [gcn_W0, gcn_W1]
        x1, x2 = (x, x)
        for i in range(LAYERS):
            W, a_s, a_d = gat_params[i]
            x1 = _gat_layer(x1, src, dst, W, a_s, a_d, concat=i != LAYERS - 1)
            x2 = _rel_gcn_layer(x2, src, dst, edge_weight, gcn_params[i])
        return jnp.maximum(x1, x2)

    def _L3_gnn_ref(x, edge_index, t, init_weight, root_weight, bias):
        import jax, jax.numpy as jnp
        import numpy as np
        STEP = 10

        def _diffusion(x, edge_index, t):
            N = x.shape[0]
            self_loop = jnp.arange(N, dtype=edge_index.dtype)
            row = jnp.concatenate([edge_index[0], self_loop])
            col = jnp.concatenate([edge_index[1], self_loop])
            deg = jax.ops.segment_sum(jnp.ones_like(col, x.dtype), col, num_segments=N)
            dinv = deg ** (-0.5)
            norm = dinv[row] * dinv[col]
            t_norm = jax.nn.softmax(t, axis=0)

            def step(h, _):
                h = jax.ops.segment_sum(norm[:, None] * h[row], col, num_segments=N)
                return (h, h)
            _, hs = jax.lax.scan(step, x, None, length=STEP - 1)
            return t_norm[0] * x + jnp.einsum('kf,knf->nf', t_norm[1:], hs)
        y = _diffusion(x, edge_index, t)
        out = jnp.einsum('nf,kfg->kng', y, init_weight)
        out = out + jnp.einsum('nf,kfg->kng', y, root_weight[0])
        out = out + bias[0]
        out = jax.nn.relu(out)
        return out.mean(axis=0)
    edge_index = jnp.stack([src, dst])
    h = jnp.maximum(_layernorm(x, axis=-1), 0.0)
    x = x + _L0_gnn_ref(h, src, dst, edge_weight, L0_gnn_weight, L0_gnn_bias)
    h = jnp.maximum(_layernorm(x, axis=-1), 0.0)
    x = x + _L1_gnn_ref(h, edge_index, L1_gnn_Wl, L1_gnn_bl, L1_gnn_Wr, L1_gnn_br)
    h = jnp.maximum(_layernorm(x, axis=-1), 0.0)
    x = x + _L2_gnn_ref(h, edge_index, edge_weight, L2_gnn_gat_W0, L2_gnn_gat_a0_src, L2_gnn_gat_a0_dst, L2_gnn_gat_W1, L2_gnn_gat_a1_src, L2_gnn_gat_a1_dst, L2_gnn_gcn_W0, L2_gnn_gcn_W1)
    h = jnp.maximum(_layernorm(x, axis=-1), 0.0)
    x = x + _L3_gnn_ref(h, edge_index, L3_gnn_t, L3_gnn_init_weight, L3_gnn_root_weight, L3_gnn_bias)
    return x

_drawn_inputs = setup_inputs


def setup_inputs(seed=0):
    import zlib

    import numpy as np

    out = dict(_drawn_inputs(seed))
    spreads = {'L3_gnn_bias': (0.0, 0.317)}
    factors = {'L0_gnn_bias': 2.738,
     'L1_gnn_bl': 200.0,
     'L1_gnn_br': 200.0,
     'L2_gnn_gat_a0_src': 198.825,
     'L2_gnn_gat_a0_dst': 200.0,
     'L2_gnn_gat_a1_src': 200.0,
     'L2_gnn_gat_a1_dst': 200.0,
     'L3_gnn_t': 43.495,
     'L1_gnn_Wr': 2.679,
     'L1_gnn_Wl': 4.204}
    for name, (base, spread) in spreads.items():
        noise = np.random.default_rng([zlib.crc32(name.encode()), seed]).standard_normal(out[name].shape)
        drawn = base * np.exp(spread * noise) if base else spread * noise
        out[name] = jnp.asarray(drawn.astype(out[name].dtype))
    for name, factor in factors.items():
        out[name] = (out[name] * factor).astype(out[name].dtype)
    return out
```

```python
from contextlib import ExitStack

import concourse.bass as bass
from concourse import mybir

F32, BF16 = mybir.dt.float32, mybir.dt.bfloat16
I32, U32, I16 = mybir.dt.int32, mybir.dt.uint32, mybir.dt.int16
ALU = mybir.AluOpType
ACT = mybir.ActivationFunctionType
AX_X = mybir.AxisListType.X

P = 128
D = 128
N = 3125
NB = -(-N // P)
NP = NB * P
E = 50000
NC = 392
WIN = 32
H = 8
BC = 8
NBATCH = NC // BC
BIG = 1e30
STEPS = 10
GUARD = 5000


class Lane:

    def __init__(self, sem):
        self.sem, self.count, self.ops, self.waited = sem, 0, [], {}

    def wait(self, *tokens):
        for token in tokens:
            if token is None:
                continue
            sem, value = token
            if self.waited.get(id(sem), 0) < value:
                self.waited[id(sem)] = value
                self.ops.append(lambda e, s=sem, v=value: e.wait_ge(s, v))

    def do(self, make, *waits):
        self.wait(*waits)
        self.count += 1
        self.ops.append(lambda e: make(e).then_inc(self.sem, 1))
        return (self.sem, self.count)

    def quiet(self, make, *waits):
        self.wait(*waits)
        self.ops.append(make)

    def last(self):
        return (self.sem, self.count)

    def chain(self, make, *waits):
        return self.do(make, self.last(), *waits)


class Landing:

    def __init__(self, sem):
        self.sem, self.count = sem, 0

    def dma(self, lane, make, *waits):
        lane.wait(*waits)
        self.count += 16
        lane.ops.append(lambda e: make(e).then_inc(self.sem, 16))
        return (self.sem, self.count)

    def last(self):
        return (self.sem, self.count) if self.count else None


class Serial:

    def __init__(self, turn_sems, landed):
        self.turns, self.landed, self.items = turn_sems, landed, []
        self.at = self.items

    def step(self, lane, make):
        self.at.append((lane, make, 0))

    def pool_dma(self, lane, make):
        self.at.append((lane, make, 1))

    def loop(self, count, fill):
        outer, body = self.at, []
        self.at = body
        fill()
        self.at = outer
        outer.append((count, body))

    @staticmethod
    def head(items):
        return Serial.head(items[0][1]) if len(items[0]) == 2 else items[0][0]

    def lanes_of(self, items):
        return {y for x in items for y in (self.lanes_of(x[1]) if len(x) == 2 else {x[0]})}

    def emit(self, items, after, put):
        for k, item in enumerate(items):
            nxt = self.head(items[k + 1:]) if k + 1 < len(items) else after
            if len(item) == 2:
                count, body = item
                assert self.head(body) is nxt
                inner = {}
                self.emit(body, nxt, lambda lane, op: inner.setdefault(id(lane), []).append(op))
                for lane in self.lanes_of(body):
                    def run(e, i, count=count, ops=inner[id(lane)]):
                        with e.Fori(0, count) as j:
                            for op in ops:
                                op(e, j)
                    put(lane, run)
            else:
                lane, make, by_pool_dma = item
                turn, give = self.turns[id(lane)], self.turns[id(nxt)]

                def run(e, i, make=make, turn=turn, give=give, landed=self.landed if by_pool_dma else None):
                    e.wait_ge(turn, 16)
                    e.sem_clear(turn)
                    if landed is None:
                        make(e, i).then_inc(give, 16)
                    else:
                        make(e, i).then_inc(landed, 16)
                        e.wait_ge(landed, 16)
                        e.dma_reset(range(landed.num, landed.num + 1))
                        e.sem_clear(landed)
                        e.sem_inc(give, 16)
                put(lane, run)

    def close(self, lane):
        assert self.head(self.items) is lane
        turn = self.turns[id(lane)]
        lane.ops.append(lambda e: e.sem_inc(turn, 16))
        self.emit(self.items, lane, lambda l, op: l.ops.append(lambda e: op(e, None)))
        lane.ops.append(lambda e: e.wait_ge(turn, 16))
        lane.ops.append(lambda e: e.sem_clear(turn))


def build(nc, a, out, *_):
    ctx = ExitStack()
    with ctx:
        sem = lambda name: ctx.enter_context(nc.semaphore(name))
        WORDS = 53200
        CW = NB * NP // 2
        arena = ctx.enter_context(nc.sbuf_tensor("arena", [P, WORDS], F32))
        banks = ctx.enter_context(nc.psum_tensor("banks", [P, 8, 512], F32))

        def at(word, shape, dt=F32, parts=P):
            n = 1
            for s in shape:
                n *= s
            w = n if dt in (F32, I32, U32) else -(-n // 2)
            assert word + w <= WORDS, (word, w)
            v = arena[0:parts, word:word + w]
            if dt != F32:
                v = v.bitcast(dt)
            if len(shape) == 2:
                v = v.rearrange("p (a b) -> p a b", b=shape[1])
            if len(shape) == 3:
                v = v.rearrange("p (a b c) -> p a b c", b=shape[1], c=shape[2])
            return v

        class Space:

            def __init__(self, word, end=WORDS):
                self.word, self.end = word, end

            def get(self, shape, dt=F32, parts=P):
                n = 1
                for s in shape:
                    n *= s
                v = at(self.word, shape, dt, parts)
                self.word += n if dt in (F32, I32, U32) else -(-n // 2)
                assert self.word <= self.end, "the arena is full"
                return v

        sp, act, pool = Lane(sem("sp")), Lane(sem("act")), Lane(sem("pool"))
        dve, pe = Lane(sem("dve")), Lane(sem("pe"))
        lanes = [sp, act, pool, dve, pe]
        turn_sems = {id(l): sem(f"turn_{n}") for n, l in zip(("sp", "act", "pool", "dve", "pe"), lanes)}
        pool_landed = sem("pool_landed")
        ctx.enter_context(nc.allow_non_contiguous_dma(reason="columns of single words, in small numbers"))
        landings = []

        named = {}

        def landing(name):
            if name not in named:
                named[name] = Landing(sem(name))
                landings.append(named[name])
            return named[name]

        def barrier():
            for lane in lanes:
                for other in lanes:
                    if other.count:
                        lane.wait(other.last())
                for x in landings:
                    lane.wait(x.last())

        def dram(name, shape, dt=F32):
            return nc.dram_tensor(name, shape, dt).ap()

        h_table = dram("h_table", [NP, D])
        x_rows = dram("x_rows", [NP, D])
        h_rows = dram("h_rows", [NP, D])
        gat0_table = dram("gat0_table", [NP, D + H])
        gat1_table = dram("gat1_table", [NP, 2 * D + H])
        ed_table = [dram(f"ed_table{i}", [NP, H]) for i in range(2)]
        adj_rows = dram("adj_rows", [P, CW])
        dst_flat = dram("dst_flat", [1, NC * P + 2], I32)
        src_flat = dram("src_flat", [1, NC * P + 2], I32)
        weight_flat = dram("weight_flat", [1, NC * P + 2])

        def blocks(ap):
            return ap.rearrange("(b p) f -> p b f", p=P)

        common, branches = {}, {}

        def snapshot():
            return ({id(l): (l.count, dict(l.waited)) for l in lanes}, {id(x): x.count for x in landings})

        def take(into):
            for l in lanes:
                into[id(l)] = l.ops
                l.ops = []

        def finish():
            with nc.Block() as block:
                for deco, lane in ((block.sync, sp), (block.scalar, act), (block.gpsimd, pool), (block.vector, dve), (block.tensor, pe)):
                    def body(e, lane=lane):
                        for op in common[id(lane)]:
                            op(e)
                        spread = e.alloc_register("spread")
                        e.reg_load(spread, FLAG[0:1, 0:1])
                        with e.If_eq(spread, 0):
                            for op in branches["regular"][id(lane)]:
                                op(e)
                        with e.Else():
                            for op in branches["any"][id(lane)]:
                                op(e)
                    deco(body)

        keep = Space(CW)
        wide = keep.get([3 * P])
        ident = wide[:, P:2 * P]
        identb = keep.get([P], BF16)
        ones = keep.get([P])
        onesb = keep.get([2], BF16)
        iota_w = keep.get([WIN])
        quad_row = keep.get([1])
        quad_mask = keep.get([4])
        tables_at = keep.word
        SRC = keep.get([NC], I32)
        REL = keep.get([NC])
        WT = keep.get([NC])
        NPAIR = NC // 2
        FIP = keep.get([NPAIR], I32)
        BND = keep.get([NPAIR + 1])
        EDI = keep.get([NC // 4], I32)
        FLAG = keep.get([1], I32)
        keep_end = keep.word
        C = at(0, [NB, NP], BF16)
        CF = at(0, [CW])
        ACC0 = at(keep_end, [NP])
        AGG = at(keep_end, [NP])
        odeg = at(keep_end + NP + NB * 3 * D // 2, [NB])

        ld = landing("ld")
        ld2 = landing("ld2")
        st = landing("st")

        tmpi = Space(keep_end)
        ti = tmpi.get([WIN], I32)
        tq = tmpi.get([1], I32)
        tp = tmpi.get([1], I32)
        tpf = tmpi.get([1])
        pool.do(lambda e: e.memset(wide, 0.0))
        pool.chain(lambda e: e.affine_select(out=wide, in_=wide, compare_op=ALU.not_equal, fill=1.0, base=P,
                                             pattern=[[-1, 3 * P]], channel_multiplier=1))
        pool.do(lambda e: e.memset(ones, 1.0))
        pool.do(lambda e: e.memset(onesb, 1.0))
        pool.do(lambda e: e.iota(ti, [[1, WIN]], base=0, channel_multiplier=0))
        pool.do(lambda e: e.iota(tq, [[0, 1]], base=0, channel_multiplier=1))
        pool.do(lambda e: e.iota(tp, [[0, 1]], base=0, channel_multiplier=1))
        c0 = pool.last()
        dve.do(lambda e: e.tensor_copy(identb, ident), c0)
        dve.do(lambda e: e.tensor_copy(iota_w, ti))
        dve.chain(lambda e: e.tensor_single_scalar(tq, tq, WIN - 1, ALU.bitwise_and))
        dve.chain(lambda e: e.tensor_copy(quad_row, tq))
        dve.chain(lambda e: e.tensor_copy(tpf, tp))
        dve.chain(lambda e: e.tensor_tensor(tpf, tpf, quad_row, ALU.subtract))
        dve.chain(lambda e: e.tensor_scalar(quad_mask, iota_w[:, 0:4], float(WIN), tpf, ALU.mult, ALU.is_equal))

        T = NC // P + 1
        s0 = Space(tmpi.word)
        raw = {k: s0.get([T, P], F32 if k == "w" else I32) for k in "sdw"}
        sf, df, rf = s0.get([T, P]), s0.get([T, P]), s0.get([T, P])
        FB = s0.get([NC])
        fills = {"s": N, "d": N, "w": 0.0}
        full = E // P
        for k in "sdw":
            pool.do(lambda e, v=raw[k][:, T - 1, :], x=fills[k]: e.memset(v, x))
        srcs = {"s": a["src"], "d": a["dst"], "w": a["edge_weight"]}
        tok = []
        for i, k in enumerate("sdw"):
            z = landing(f"edges_{k}")
            v = srcs[k]
            body = v[0:(T - 1) * P * P].rearrange("(t p e) -> p t e", p=P, e=P)
            rest = v[(T - 1) * P * P:full * P].rearrange("(p e) -> p e", e=P)
            tail = v[full * P:E].rearrange("(p e) -> p e", p=1)
            nf = full - (T - 1) * P
            z.dma(sp, lambda e, b=body, k=k: e.dma_start(raw[k][:, 0:T - 1, :], b), pool.last())
            z.dma(sp, lambda e, b=rest, k=k, nf=nf: e.dma_start(raw[k][0:nf, T - 1, :], b))
            tok.append(z.dma(sp, lambda e, b=tail, k=k, nf=nf: e.dma_start(raw[k][nf:nf + 1, T - 1, 0:E - full * P], b)))
        dve.do(lambda e: e.tensor_copy(sf, raw["s"]), tok[0])
        dve.do(lambda e: e.tensor_copy(df, raw["d"]), tok[1])
        for t in range(T):
            dve.do(lambda e, t=t: e.tensor_scalar(rf[:, t, :], df[:, t, :], df[:, t, 0:1], None, ALU.subtract), dve.last())
        tabs = dve.last()
        gtile = s0.get([2], I32)
        pool.do(lambda e: e.memset(gtile, GUARD))
        nr = NC - (T - 1) * P
        for i, (k, table) in enumerate((("s", src_flat), ("d", dst_flat), ("w", weight_flat))):
            flat = table[0:1, :]
            guard = gtile[0:1, 0:1] if k != "w" else gtile[0:1, 0:1].bitcast(F32)
            st.dma(sp, lambda e, k=k, flat=flat: e.dma_start(flat[:, 1:1 + (T - 1) * P * P].rearrange("o (t p e) -> (o p) t e", p=P, e=P), raw[k][:, 0:T - 1, :]), tok[i], pool.last())
            st.dma(sp, lambda e, k=k, flat=flat: e.dma_start(flat[:, 1 + (T - 1) * P * P:1 + NC * P].rearrange("o (p e) -> (o p) e", e=P), raw[k][0:nr, T - 1, :]))
            st.dma(sp, lambda e, flat=flat, guard=guard: e.dma_start(flat[:, 0:1], guard))
            st.dma(sp, lambda e, flat=flat, guard=guard: e.dma_start(flat[:, NC * P + 1:NC * P + 2], guard))
        prev = {}
        for i, (v, o) in enumerate(((sf, SRC), (rf, REL), (raw["w"], WT))):
            for t in range(T):
                n = min(P, NC - t * P)
                bk = (i * T + t) % 4
                tr = pe.do(lambda e, v=v, t=t, n=n, bk=bk: e.transpose(banks[:, bk, 0:n], v[0:n, t, :], ident[0:n, 0:n]),
                           tabs, tok[2], c0, prev.get(bk))
                prev[bk] = dve.do(lambda e, o=o, t=t, n=n, bk=bk: e.tensor_copy(o[:, t * P:t * P + n], banks[:, bk, 0:n]), tr)
        for t in range(T):
            n = min(P, NC - t * P)
            tr = pe.do(lambda e, t=t, n=n: e.matmul(banks[:, 4, t * P:t * P + n], df[0:n, t, 0:1].broadcast_to([n, P]),
                                                    ident[0:n, 0:n], start=True, stop=True))
        dve.do(lambda e: e.tensor_copy(FB, banks[:, 4, 0:NC]), tr)
        dve.chain(lambda e: e.tensor_copy(FIP, FB[:, 0:NC:2]))
        for j in range(4):
            q = slice(32 * j, 32 * j + 32)
            dve.do(lambda e, j=j, q=q: e.tensor_scalar(EDI[q, :], FB[q, j // 2 * 2:NC:4], quad_row[q, :], None, ALU.add), dve.last())
        bad = s0.get([8])
        cmp = s0.get([T, P])
        step = s0.get([NC])
        pair = s0.get([NC // 2])

        def count_of(k, v, make):
            dve.chain(make)
            dve.chain(lambda e, k=k, v=v: e.tensor_reduce(bad[:, k:k + 1], v, AX_X if len(v.shape) == 2 else mybir.AxisListType.XY, ALU.add))

        dve.do(lambda e: e.memset(bad, 0.0))
        count_of(0, cmp[:, :, 1:P], lambda e: e.tensor_tensor(cmp[:, :, 1:P], df[:, :, 1:P], df[:, :, 0:P - 1], ALU.is_lt))
        count_of(1, cmp, lambda e: e.tensor_scalar(cmp, rf, float(WIN), None, ALU.is_ge))
        dve.chain(lambda e: e.tensor_tensor(step[:, 0:NC - 1], FB[:, 1:NC], FB[:, 0:NC - 1], ALU.subtract))
        late = cmp.rearrange("p t e -> p (t e)")[:, 0:NC - 1]
        count_of(2, late, lambda e: e.tensor_tensor(late, REL[:, 0:NC - 1], step[:, 0:NC - 1], ALU.is_gt))
        count_of(3, late, lambda e: e.tensor_scalar(late, step[:, 0:NC - 1], 0.0, None, ALU.is_le))
        dve.do(lambda e: e.memset(BND, 0.0))
        dve.chain(lambda e: e.tensor_tensor(BND[:, 1:NPAIR], REL[:, 1:NC - 1:2], step[:, 1:NC - 1:2], ALU.is_equal))
        dve.chain(lambda e: e.tensor_tensor(REL[:, 1:NC:2], REL[:, 1:NC:2], step[:, 0:NC:2], ALU.add))
        count_of(4, late, lambda e: e.tensor_scalar(late, REL[:, 1:NC], float(WIN), None, ALU.is_ge))
        dve.chain(lambda e: e.tensor_tensor(pair[:, 0:NPAIR - 1], FB[:, 2:NC:2], FB[:, 0:NC - 2:2], ALU.subtract))
        count_of(5, pair[:, 0:NPAIR - 1], lambda e: e.tensor_scalar(pair[:, 0:NPAIR - 1], pair[:, 0:NPAIR - 1], float(WIN), None, ALU.is_gt))
        dve.chain(lambda e: e.tensor_scalar(bad[:, 6:7], FB[:, 0:1], 0.0, None, ALU.not_equal))
        dve.chain(lambda e: e.tensor_reduce(bad[:, 7:8], bad[:, 0:7], AX_X, ALU.add))
        m = pe.do(lambda e: e.matmul(banks[:, 5, 0:1], ones, bad[:, 7:8], start=True, stop=True), dve.last())
        dve.do(lambda e: e.tensor_copy(FLAG, banks[:, 5, 0:1]), m)
        barrier()

        def layer_norm(X, Y, space, n=NB, ready=None):
            dve.wait(dve.last())
            stats, mv, rs = space.get([NB, 6]), space.get([NB, 2]), space.get([NB])
            for b in range(n):
                dve.do(lambda e, b=b: e.bn_stats(stats[:, b, :], X[:, b, :]), ready)
            t = dve.last()
            for b in range(n):
                dve.do(lambda e, b=b: e.bn_aggr(mv[:, b, :], stats[:, b, :]), t)
            dve.chain(lambda e: e.tensor_scalar_add(rs, mv[:, :, 1], 1e-5))
            r = act.do(lambda e: e.activation(rs, rs, ACT.Sqrt), dve.last())
            dve.chain(lambda e: e.reciprocal(rs, rs), r)
            t = dve.last()
            for b in range(n):
                dve.do(lambda e, b=b: e.tensor_scalar(Y[:, b, :], X[:, b, :], mv[:, b, 0:1], rs[:, b:b + 1],
                                                      ALU.subtract, ALU.mult), t)
            return dve.chain(lambda e: e.tensor_scalar_max(Y, Y, 0.0))

        def load_x(X):
            z = dve.do(lambda e: e.memset(X[:, NB - 1, :], 0.0))
            f = N // P
            ld.dma(sp, lambda e: e.dma_start(X[:, 0:f, :], a["x"][0:f * P, :].rearrange("(b p) f -> p b f", p=P)), z)
            return ld.dma(sp, lambda e: e.dma_start(X[0:N - f * P, f, :], a["x"][f * P:N, :]))

        def first_norm():
            s1 = Space(keep_end)
            X, Hh = s1.get([NB, D]), s1.get([NB, D])
            ready = load_x(X)
            done = layer_norm(X, Hh, s1, ready=ready)
            st.dma(sp, lambda e: e.dma_start(blocks(h_table), Hh), done)
            barrier()

        first_norm()
        gl = [landing(f"g{i}") for i in range(40)]
        env = {}

        def firsts(lane, c0, n):
            env["tags"] = tag = env.get("tags", 0) + 1

            def op(e):
                regs = [e.alloc_register(f"first{tag}_{k}") for k in range(n)]
                e.reg_load(regs, FIP[0:1, c0:c0 + n])
                for k, r in enumerate(regs):
                    env[(id(lane), c0 + k)] = e.snap(r, donate=True, min_val=0, max_val=N)
                env[(id(lane), "regs")] = regs
            lane.ops.append(op)

        def release(lane):
            def op(e):
                for r in env[(id(lane), "regs")]:
                    e.free_register(r)
            lane.ops.append(op)

        def window(lane, ap, c):
            v = env[(id(lane), c)]
            if len(ap.shape) == 3:
                return ap[:, :, bass.ds(v, WIN)]
            return ap[:, bass.ds(v, WIN)]

        def layer0_edges():
            s2 = Space(keep_end)
            s2.get([NP])
            R, RX, RB = 16, 4, 4
            G = s2.get([R, D])
            S = s2.get([R, WIN])
            BY_LO = s2.get([RX, P], BF16)
            BY_HI_D = s2.get([RX, NB * WIN], BF16)
            BY_HI = s2.get([RB, WIN], BF16)
            columns = s2.get([NB * WIN], I16)
            LO, HI, KEY = s2.get([NC]), s2.get([NC]), s2.get([NC])
            LOI, HII = s2.get([NC], I32), s2.get([NC], I32)
            WB = s2.get([NPAIR])
            tail = N + 1
            dve.do(lambda e: e.memset(ACC0[:, tail:NP], 0.0))
            dve.do(lambda e: e.memset(C[:, :, tail:NP], 0.0))
            pool.do(lambda e: e.iota(columns, [[1, NB * WIN]], base=0, channel_multiplier=0))
            dve.do(lambda e: e.tensor_single_scalar(LOI, SRC, P - 1, ALU.bitwise_and))
            dve.do(lambda e: e.tensor_single_scalar(HII, SRC, 7, ALU.logical_shift_right))
            dve.do(lambda e: e.tensor_tensor(WB[:, 1:NPAIR], WT[:, 1:NC - 1:2], BND[:, 1:NPAIR], ALU.mult))
            dve.chain(lambda e: e.tensor_copy(LO, LOI))
            dve.do(lambda e: e.tensor_copy(HI, HII))
            dve.chain(lambda e: e.scalar_tensor_tensor(KEY, HI, float(WIN), REL, ALU.mult, ALU.add))
            barrier()
            T = {}
            get = T.get

            def chunk(c):
                p, k, kx = c // 2, c % R, c % RX
                g = gl[k].dma(pool, lambda e: e.indirect_dma_start(
                    G[:, k, :], None, h_table, bass.IndirectOffsetOnAxis(ap=SRC[:, c:c + 1].bitcast(U32), axis=0)), get(("free", c - R)))
                dve.do(lambda e: e.tensor_scalar(BY_LO[:, kx, :], columns[:, 0:P], LO[:, c:c + 1], None, ALU.is_equal), get(("free", c - RX)))
                x = dve.do(lambda e: e.tensor_scalar(BY_HI_D[:, kx, :], columns, KEY[:, c:c + 1], None, ALU.is_equal))
                w = dve.do(lambda e: e.tensor_scalar(S[:, k, :], iota_w, REL[:, c:c + 1], WT[:, c:c + 1], ALU.is_equal, ALU.mult))
                if c % 2 and p < NPAIR - 1:
                    T["shared", p] = dve.do(lambda e: e.tensor_scalar(BY_HI[:, p % RB, 0:NB], columns[:, 0:NB], HI[:, c:c + 1], BND[:, p + 1:p + 2],
                                                                      ALU.is_equal, ALU.mult), get(("free", 2 * (p - RB) + 1)))
                q = p % 2
                B0 = 512 // WIN
                cuts = ((0, B0), (B0, NB))
                pa = banks[:, 4 + q, 0:WIN]

                def counts(at_bank, lhs, rhs, out, **kw):
                    return lambda e: e.matmul(out, lhs, rhs, skip_group_check=True, **kw)

                even = c % 2 == 0
                for m, (b0, b1) in enumerate(cuts):
                    pe.quiet(counts(m, BY_LO[:, kx, :], BY_HI_D[:, kx, b0 * WIN:b1 * WIN], banks[:, 2 * q + m, 0:(b1 - b0) * WIN],
                                    start=even, stop=not even), x, get(("adj", p - 2)))
                mm = pe.do(lambda e: e.matmul(pa, G[:, k, :], S[:, k, :], start=even, stop=not even, skip_group_check=True), g, w, get(("acc", p - 2)))
                if even:
                    T["free", c] = mm
                    if p:
                        kb = (c - 1) % R
                        for m, (b0, b1) in enumerate(cuts):
                            o = banks[:, 2 * q + m, 0:(b1 - b0) * WIN].rearrange("p (b w) -> p b w", w=WIN)[:, :, 0]
                            pe.quiet(counts(m, BY_LO[:, (c - 1) % RX, :], BY_HI[:, (p - 1) % RB, b0:b1], o, start=False, stop=False), T["shared", p - 1])
                        T["free", c - 1] = pe.do(lambda e: e.matmul(pa[:, 0:1], G[:, kb, :], WB[:, p:p + 1], start=False, stop=False, skip_group_check=True))
                else:
                    T["mm", p] = mm

            def copy_windows(p):
                q = p % 2
                pc = banks[:, 2 * q:2 * q + 2, :].rearrange("p k (b w) -> p (k b) w", w=WIN)[:, 0:NB, :]
                T["adj", p] = act.do(lambda e: e.activation(window(act, C, p), pc, ACT.Copy), T["mm", p], get(("adj", p - 1)))
                T["acc", p] = act.do(lambda e: e.activation(window(act, ACC0, p), banks[:, 4 + q, 0:WIN], ACT.Copy), get(("acc", p - 1)))

            for c in range(NC):
                if c % 8 == 0:
                    firsts(act, c // 2, 4)
                chunk(c)
                if c % 2 == 1:
                    copy_windows(c // 2)
                if c % 8 == 7:
                    release(act)
            barrier()
            adj_saved = landing("adj_saved")
            adj_saved.dma(act, lambda e: e.dma_start(adj_rows, CF))

        def groups(width=4):
            return [(b, min(width, NB - b)) for b in range(0, NB, width)]

        def load_row(z, v, row):
            return z.dma(sp, lambda e: e.dma_start(v, row.partition_broadcast(P)))

        def row_of(ap):
            while len(ap.shape) > 1:
                ap = ap[0]
            return ap

        def layer0_nodes():
            s3 = Space(keep_end)
            s3.get([NP])
            X, Hh = s3.get([NB, D]), s3.get([NB, D])
            W0, B0 = s3.get([D]), s3.get([D])
            ld2.dma(sp, lambda e: e.dma_start(W0, a["L0_gnn_weight"]))
            wready = load_row(ld2, B0, a["L0_gnn_bias"])
            xready = load_x(X)
            freed = {}
            for g, (b0, n) in enumerate(groups()):
                bk = g % 4
                for b in range(b0, b0 + n):
                    m = pe.do(lambda e, b=b, b0=b0, bk=bk: e.matmul(
                        banks[:, bk, (b - b0) * D:(b - b0 + 1) * D], ACC0[:, b * P:(b + 1) * P], W0, start=True, stop=True),
                        wready, freed.get(g - 4))
                xs = X[:, b0:b0 + n, :]
                u = dve.do(lambda e, xs=xs, bk=bk, n=n: e.tensor_tensor(
                    xs, xs, banks[:, bk, 0:n * D].rearrange("p (b f) -> p b f", f=D), ALU.add), m, xready)
                freed[g] = u
            dve.chain(lambda e: e.tensor_tensor(X, X, B0.unsqueeze(1).broadcast_to([P, NB, D]), ALU.add))
            done = layer_norm(X, Hh, s3)
            st.dma(sp, lambda e: e.dma_start(blocks(x_rows), X), done)
            st.dma(sp, lambda e: e.dma_start(blocks(h_rows), Hh))
            barrier()


        def split3(src, parts, tmp, *waits):
            hi, mid, lo = parts
            dve.do(lambda e: e.tensor_copy(hi, src), *waits)
            dve.chain(lambda e: e.tensor_tensor(tmp, src, hi, ALU.subtract))
            dve.chain(lambda e: e.tensor_copy(mid, tmp))
            return dve.chain(lambda e: e.tensor_tensor(lo, tmp, mid, ALU.subtract))

        def layer1_sums():
            s4 = Space(keep_end)
            s4.get([NP])
            U = s4.get([NB, 3 * D], BF16)
            s4.get([NB])
            Hl = s4.get([5, D])
            ct_at = s4.word
            tmp = s4.get([5, D])
            NH = [13, 12]
            for q in range(0, NB, 5):
                hr = ld.dma(sp, lambda e, q=q: e.dma_start(Hl, blocks(h_rows)[:, q:q + 5, :]), dve.last())
                split3(Hl, [U[:, q:q + 5, k * D:(k + 1) * D] for k in range(3)], tmp, hr)
            udone = dve.last()
            s4 = Space(ct_at)
            CT = [s4.get([NH[0] * P], BF16) for _ in range(2)]
            it = 0
            ct_free, bank_free = {}, {}
            agg_free = None
            for half in range(2):
                nh = NH[half]
                sb0 = half * NH[0]
                w = nh * P
                for db in range(NB):
                    k = it % 2
                    tb = 4 + 2 * k
                    for i in range(nh):
                        bank, col = tb + i // 8, (i % 8) * P
                        m = pe.do(lambda e, i=i, bank=bank, col=col, db=db, sb0=sb0: e.transpose(
                            banks[:, bank, :].bitcast(BF16)[:, col:col + P], C[:, sb0 + i, db * P:(db + 1) * P], identb),
                            bank_free.get(it - 2))
                    e1 = act.do(lambda e, k=k, tb=tb: e.activation(CT[k][:, 0:8 * P], banks[:, tb, :].bitcast(BF16), ACT.Copy),
                                m, ct_free.get(it - 2), udone)
                    e2 = dve.do(lambda e, k=k, tb=tb, w=w: e.tensor_copy(CT[k][:, 8 * P:w], banks[:, tb + 1, :].bitcast(BF16)[:, 0:w - 8 * P]),
                                m, ct_free.get(it - 2), udone)
                    if it % 2 == 0:
                        dve.do(lambda e, b=it // 2: e.tensor_reduce(odeg[:, b:b + 1], C[:, b, :], AX_X, ALU.add))
                    pend = (e1, e2)
                    def products(it, half, db, w, pend):
                        k = it % 2
                        for j in range(3):
                            for c in range(0, w, 512):
                                n = min(512, w - c)
                                m = pe.do(lambda e, j=j, c=c, n=n, db=db, k=k: e.matmul(
                                    banks[:, c // 512, 0:n], U[:, db, j * D:(j + 1) * D], CT[k][:, c:c + n],
                                    start=(db == 0 and j == 0), stop=(db == NB - 1 and j == 2), skip_group_check=True), *pend, udone, agg_free)
                        ct_free[it] = m
                        return m
                    bank_free[it] = None
                    if db:
                        products(it - 1, half, db - 1, w, prevp)
                    prevp = pend
                    bank_free[it] = e1
                    bank_free[it + 0.5] = e2
                    it += 1
                    pe.wait(bank_free.get(it - 2), bank_free.get(it - 1.5))
                m = products(it - 1, half, NB - 1, w, prevp)
                for c in range(0, w, 512):
                    n = min(512, w - c)
                    agg_free = act.do(lambda e, c=c, n=n, sb0=sb0: e.activation(AGG[:, sb0 * P + c:sb0 * P + c + n], banks[:, c // 512, 0:n], ACT.Copy), m)
            barrier()


        def layer1_nodes():
            s5 = Space(keep_end + NP)
            X = s5.get([NB, D])
            s5 = Space(keep_end + 2 * NP, keep_end + NP + NB * 3 * D // 2)
            Wl, Wr, Bl, Br = (s5.get([D]) for _ in range(4))
            rd, nrm = s5.get([NB]), s5.get([NB])
            t2 = [s5.get([4, D])]
            s5 = Space(keep_end + NP + NB * 3 * D // 2 + NB)
            Hl = [s5.get([4, D]) for _ in range(2)]
            Ht = [s5.get([4 * D]) for _ in range(2)]
            ld2.dma(sp, lambda e: e.dma_start(Wl, a["L1_gnn_Wl"]))
            ld2.dma(sp, lambda e: e.dma_start(Wr, a["L1_gnn_Wr"]))
            load_row(ld2, Bl, a["L1_gnn_bl"])
            wready = load_row(ld2, Br, a["L1_gnn_br"])
            xready = ld.dma(sp, lambda e: e.dma_start(X, blocks(x_rows)))
            dve.do(lambda e: e.tensor_tensor(Bl, Bl, Br, ALU.add), wready)
            dve.do(lambda e: e.tensor_scalar_max(rd, odeg, 1.0))
            dve.chain(lambda e: e.reciprocal(rd, rd))
            hl = [landing("hl0"), landing("hl1")]
            ht_free, hl_free, bank_free, t2_free = {}, {}, {}, None
            for g, (b0, n) in enumerate(groups()):
                k = g % 2
                hr = hl[k].dma(sp, lambda e, b0=b0, n=n, k=k: e.dma_start(Hl[k][:, 0:n, :], blocks(h_rows)[:, b0:b0 + n, :]), hl_free.get(g - 2))
                for i in range(n):
                    m = pe.do(lambda e, i=i, k=k: e.transpose(banks[:, 6 + k, i * P:(i + 1) * P], Hl[k][:, i, :], ident), hr, ht_free.get(g - 2))
                hl_free[g] = m
                hc = act.do(lambda e, k=k, n=n: e.activation(Ht[k][:, 0:n * P], banks[:, 6 + k, 0:n * P], ACT.Copy), m, ht_free.get(g - 2))
                for i in range(n):
                    b = b0 + i
                    pe.do(lambda e, i=i, k=k: e.matmul(banks[:, k, i * D:(i + 1) * D], Ht[k][:, i * P:(i + 1) * P], Wl, start=True, stop=True), hc, wready, bank_free.get(g - 2))
                    m = pe.do(lambda e, i=i, k=k, b=b: e.matmul(banks[:, 2 + k, i * D:(i + 1) * D], AGG[:, b * P:(b + 1) * P], Wr, start=True, stop=True))
                ht_free[g] = m
                v = t2[0][:, 0:n, :]
                p1 = banks[:, k, 0:n * D].rearrange("p (b f) -> p b f", f=D)
                p2 = banks[:, 2 + k, 0:n * D].rearrange("p (b f) -> p b f", f=D)
                dve.do(lambda e, v=v, p2=p2, b0=b0, n=n: e.tensor_tensor(v, p2, rd[:, b0:b0 + n].unsqueeze(2).broadcast_to([P, n, D]), ALU.mult), dve.last(), m, t2_free)
                dve.chain(lambda e, v=v, p1=p1: e.tensor_tensor(v, v, p1, ALU.add))
                bank_free[g] = dve.last()
                dve.chain(lambda e, v=v, n=n: e.tensor_tensor(v, v, Bl.unsqueeze(1).broadcast_to([P, n, D]), ALU.add))
                r = dve.chain(lambda e, v=v: e.tensor_scalar_max(v, v, 0.0))
                for i in range(n):
                    sq = act.do(lambda e, i=i, b=b0 + i, k=k, v=v: e.activation(Hl[k][:, i, :], v[:, i, :], ACT.Square, accum_out=nrm[:, b:b + 1]), r)
                hl_free[g] = sq
                q = act.do(lambda e, b0=b0, n=n: e.activation(nrm[:, b0:b0 + n], nrm[:, b0:b0 + n], ACT.Sqrt), sq)
                dve.do(lambda e, b0=b0, n=n: e.tensor_scalar_add(nrm[:, b0:b0 + n], nrm[:, b0:b0 + n], 1e-6), q)
                dve.chain(lambda e, b0=b0, n=n: e.reciprocal(nrm[:, b0:b0 + n], nrm[:, b0:b0 + n]))
                dve.chain(lambda e, v=v, b0=b0, n=n: e.tensor_tensor(v, v, nrm[:, b0:b0 + n].unsqueeze(2).broadcast_to([P, n, D]), ALU.mult))
                xs = X[:, b0:b0 + n, :]
                dve.chain(lambda e, v=v, xs=xs: e.tensor_tensor(xs, xs, v, ALU.add), xready)
                t2_free = dve.last()
            barrier()
            s6 = Space(keep_end)
            H2 = s6.get([NB, D])
            s6 = Space(keep_end + 2 * NP)
            layer_norm(X, H2, s6)
            st.dma(sp, lambda e: e.dma_start(blocks(x_rows), X), dve.last())
            barrier()


        RING = 40
        ACC = at(0, [H + 1, NP])
        SACC = at(keep_end, [NP], parts=H + 1)
        ring_at = (H + 1) * NP
        X1, X2 = at(ring_at, [NB, D]), at(ring_at + NP, [NB, D])
        node_at = keep_end + NP
        gat = [{k: a[f"L2_gnn_{v}"] for k, v in (("W", f"gat_W{i}"), ("src", f"gat_a{i}_src"), ("dst", f"gat_a{i}_dst"))}
               for i in range(2)]

        def scores(i, Hn, V, ES, space):
            K = D // H if i == 0 else D
            Wg, av, pr = (space.get([H, K]) for _ in range(3))
            Ht = [space.get([4 * D]) for _ in range(2)]
            w = ld2.dma(sp, lambda e: e.dma_start(Wg, gat[i]["W"].rearrange("h f k -> f h k")), dve.last(), pe.last())
            for j, k in enumerate(("src", "dst")):
                r = ld2.dma(sp, lambda e, k=k: e.dma_start(av.rearrange("p h k -> p (h k)"), gat[i][k].rearrange("h k -> (h k)").partition_broadcast(P)), dve.last())
                dve.do(lambda e: e.tensor_tensor(pr, Wg, av, ALU.mult), r, dve.last())
                dve.chain(lambda e, j=j: e.tensor_reduce(V[:, j * H:(j + 1) * H], pr, AX_X, ALU.add))
            vt = dve.last()
            hfree, bfree = {}, {}
            for g, (b0, n) in enumerate(groups()):
                k = g % 2
                for q in range(n):
                    m = pe.do(lambda e, q=q, k=k, b0=b0: e.transpose(banks[:, 6 + k, q * P:(q + 1) * P], Hn[:, b0 + q, :], ident), vt, hfree.get(g - 2))
                hc = act.do(lambda e, k=k, n=n: e.activation(Ht[k][:, 0:n * P], banks[:, 6 + k, 0:n * P], ACT.Copy), m, bfree.get(g - 2), vt)
                hfree[g] = hc
                for q in range(n):
                    m = pe.do(lambda e, q=q, k=k: e.matmul(banks[:, 4 + k, q * 2 * H:(q + 1) * 2 * H], Ht[k][:, q * P:(q + 1) * P], V, start=True, stop=True), hc, bfree.get(g - 2))
                bfree[g] = dve.do(lambda e, k=k, n=n, b0=b0: e.tensor_copy(ES[:, b0:b0 + n, :], banks[:, 4 + k, 0:n * 2 * H].rearrange("p (b s) -> p b s", s=2 * H)), m)
            return dve.last()

        def layer2_tables0():
            H2 = at(keep_end, [NB, D])
            space = Space(keep_end + NP)
            V, ES = space.get([2 * H]), space.get([NB, 2 * H])
            done = scores(0, H2, V, ES, space)
            st.dma(sp, lambda e: e.dma_start(blocks(gat0_table)[:, :, 0:D], H2), done)
            st.dma(sp, lambda e: e.dma_start(blocks(gat0_table)[:, :, D:D + H], ES[:, :, 0:H]))
            st.dma(sp, lambda e: e.dma_start(blocks(ed_table[0]), ES[:, :, H:2 * H]))
            barrier()

        def layer2_edges(i):
            table, row = (gat0_table, D + H) if i == 0 else (gat1_table, 2 * D + H)
            space = Space(node_at)
            G = at(ring_at, [RING, row])
            R4, R3, RS = 4, 3, 4
            OH = [space.get([BC, WIN]) for _ in range(R4)]
            OT = [space.get([2 * P]) for _ in range(2)]
            EDR = [space.get([2, H]) for _ in range(R4)]
            BD = [space.get([2, 4, H]) for _ in range(2)]
            DLI = [space.get([P + 2], I32, 64) for _ in range(2)]
            DLF = [space.get([P + 2], parts=64) for _ in range(2)]
            EQ = [space.get([P + 1], parts=64) for _ in range(2)]
            MF, MN = ([space.get([P], parts=64) for _ in range(R3)] for _ in range(2))
            Z = [space.get([64]) for _ in range(2)]
            ZT = [space.get([P], parts=64) for _ in range(R3)]
            FW = space.get([P], parts=64)
            ML = [space.get([P], parts=64) for _ in range(R4)]
            MM = space.get([P], parts=64)
            DF = [space.get([P], parts=64) for _ in range(2)]
            A = [space.get([BC, H + 1]) for _ in range(R3)]
            S = [space.get([H + 1, WIN]) for _ in range(RS)]
            SB = [space.get([BC // 2, H + 1]) for _ in range(R3)]
            dve.do(lambda e: e.memset(ACC[:, :, N + 1:NP], 0.0))
            dve.do(lambda e: e.memset(SACC[:, N + 1:NP], 0.0))
            zero = dve.last()
            dl = [landing(f"dl{i}_{k}") for k in range(2)]
            edl = [landing(f"ed{i}_{k}") for k in range(2 * R4)]
            T = {}
            get = T.get

            def gathers(b):
                for g in range(2):
                    q = 2 * b + g
                    T["ed", q] = edl[q % (2 * R4)].dma(pool, lambda e, q=q, b=b, g=g: e.indirect_dma_start(
                        EDR[b % R4][:, g, :], None, ed_table[i], bass.IndirectOffsetOnAxis(ap=EDI[:, q:q + 1].bitcast(U32), axis=0)),
                        get(("bd", b - R4)))
                    for c in range(4 * q, 4 * q + 4):
                        T["g", c] = gl[c % RING].dma(pool, lambda e, c=c: e.indirect_dma_start(
                            G[:, c % RING, :], None, table, bass.IndirectOffsetOnAxis(ap=SRC[:, c:c + 1].bitcast(U32), axis=0)),
                            get(("free", c - RING)))

            def rows_of(b):
                src = dst_flat[0, b * BC * P:b * BC * P + 1]
                ap = bass.AP(tensor=dst_flat.tensor, offset=b * BC * P, ap=[[P, BC], [0, H], [1, P + 2]])
                T["dl", b] = dl[b % 2].dma(sp, lambda e, b=b, ap=ap: e.dma_start(DLI[b % 2], ap), get(("dlf", b - 2)))

            def s1(b):
                k4, k3, k2 = b % R4, b % R3, b % 2
                c0 = b * BC

                def one_hot():
                    T["oh", b] = dve.do(lambda e: e.tensor_tensor(
                        OH[k4], iota_w.unsqueeze(1).broadcast_to([P, BC, WIN]),
                        REL[:, c0:c0 + BC].unsqueeze(2).broadcast_to([P, BC, WIN]), ALU.is_equal),
                        get(("mm", c0 + BC - 1 - R4 * BC)), get(("sm", c0 + BC - 1 - R4 * BC)), get(("tr", b - R4)))
                    T["dlf", b] = dve.do(lambda e: e.tensor_copy(DLF[k2], DLI[k2]), T["dl", b], get(("flags", b - 2)))

                def turn():
                    for g in range(2):
                        T["tr", b] = pe.do(lambda e, g=g: e.transpose(
                            banks[:, 0, g * P:(g + 1) * P], OH[k4][:, 4 * g:4 * g + 4, :].rearrange("p c w -> p (c w)"), ident),
                            T["oh", b], get(("ot", b - 1)))
                    T["ot", b] = act.do(lambda e: e.activation(OT[k2], banks[:, 0, 0:2 * P], ACT.Copy), T["tr", b], get(("edm", b - 2)))

                def flags():
                    d = DLF[k2]
                    dve.do(lambda e: e.tensor_tensor(EQ[k2], d[:, 0:P + 1], d[:, 1:P + 2], ALU.not_equal), T["dlf", b], get(("bw", b - 2)))
                    dve.do(lambda e: e.tensor_scalar(MF[k3], d[:, 1:P + 1], d[:, 0:1], -BIG, ALU.not_equal, ALU.mult), get(("m", b - R3)))
                    dve.do(lambda e: e.tensor_scalar(MN[k3], d[:, 1:P + 1], d[:, P + 1:P + 2], -BIG, ALU.not_equal, ALU.mult))
                    T["flags", b] = dve.chain(lambda e: e.tensor_scalar(EQ[k2], EQ[k2], -BIG, None, ALU.mult))
                    T["aw", b] = dve.do(lambda e: e.tensor_copy(A[k3][:, :, H], WT[:, c0:c0 + BC]), get(("sg", c0 + BC - 1 - R3 * BC)), get(("sm", c0 + BC - 1 - R3 * BC)), get(("sb", b - R3)))

                def expand():
                    T["bd", b] = dve.do(lambda e: e.tensor_tensor(
                        BD[k2], EDR[k4].unsqueeze(2).broadcast_to([P, 2, 4, H]),
                        quad_mask.unsqueeze(1).unsqueeze(3).broadcast_to([P, 2, 4, H]), ALU.mult),
                        T["ed", 2 * b], T["ed", 2 * b + 1], get(("edm", b - 2)))
                    for g in range(2):
                        T["edm", b] = pe.do(lambda e, g=g: e.matmul(
                            banks[:, 1, g * 4 * H:(g + 1) * 4 * H], OT[k2][:, g * P:(g + 1) * P],
                            BD[k2][:, g, :, :].rearrange("p j h -> p (j h)"), start=True, stop=True),
                            T["ot", b], T["bd", b], get(("z", b - 1)))

                def logits():
                    s = c0 % RING
                    z = Z[k2].rearrange("p (c h) -> p c h", h=H)
                    T["z", b] = dve.do(lambda e: e.tensor_tensor(
                        z, banks[:, 1, 0:BC * H].rearrange("p (c h) -> p c h", h=H), G[:, s:s + BC, D:D + H], ALU.add),
                        T["edm", b], *[T["g", c] for c in range(c0, c0 + BC)], get(("zt", b - 2)))
                    T["zr", b] = dve.chain(lambda e: e.scalar_tensor_tensor(Z[k2], Z[k2], 0.2, Z[k2], ALU.mult, ALU.max))

                def turn_logits():
                    T["zt", b] = pe.do(lambda e: e.transpose(banks[0:64, 2, 0:P], Z[k2], ident), T["zr", b], get(("ztc", b - 1)))
                    T["ztc", b] = act.do(lambda e: e.activation(ZT[k3], banks[0:64, 2, 0:P], ACT.Copy), T["zt", b], get(("d", b - R3)), get(("bw", b - R3)))

                def scans():
                    dve.do(lambda e: e.tensor_tensor_scan(FW, EQ[k2][:, 0:P], ZT[k3], -BIG, ALU.add, ALU.max), T["ztc", b], T["flags", b], dve.last())
                    T["bw", b] = dve.do(lambda e: e.tensor_tensor_scan(ML[k4][:, ::-1], EQ[k2][:, P:0:-1], FW[:, ::-1], -BIG, ALU.add, ALU.max),
                                        dve.last(), get(("ex", b - R4 + 1)), get(("m", b - R4)))

                return [one_hot, turn, flags, expand, logits, turn_logits, scans]

            def s2(b):
                k4, k3, k2 = b % R4, b % R3, b % 2

                def exchange():
                    me = ML[k4]
                    pr = ML[(b - 1) % R4] if b else None
                    ne = ML[(b + 1) % R4] if b < NBATCH - 1 else None
                    w = (T["bw", b], get(("bw", b + 1)), get(("m", b - 1)))
                    o = banks[0:64, 3, 0:2]
                    pe.do(lambda e: e.matmul(o[:, 0:1], wide[0:64, P - H:P - H + 64], me[:, P - 1:P], start=True, stop=pr is None), *w)
                    if pr is not None:
                        pe.do(lambda e: e.matmul(o[:, 0:1], wide[0:64, P + 64 - H:P + 128 - H], pr[:, P - 1:P], start=False, stop=True))
                    T["ex", b] = pe.do(lambda e: e.matmul(o[:, 1:2], wide[0:64, P + H:P + H + 64], me[:, 0:1], start=True, stop=ne is None))
                    if ne is not None:
                        T["ex", b] = pe.do(lambda e: e.matmul(o[:, 1:2], wide[0:64, P - 64 + H:P + H], ne[:, 0:1], start=False, stop=True))

                def maxima():
                    o = banks[0:64, 3, 0:2]
                    dve.do(lambda e: e.scalar_tensor_tensor(MM, MF[k3], o[:, 0:1], ML[k4], ALU.add, ALU.max), T["ex", b], dve.last())
                    T["m", b] = dve.chain(lambda e: e.scalar_tensor_tensor(MM, MN[k3], o[:, 1:2], MM, ALU.add, ALU.max))
                    T["d", b] = dve.chain(lambda e: e.tensor_tensor(DF[k2], ZT[k3], MM, ALU.subtract), get(("p", b - 2)))

                def expo():
                    x = act.do(lambda e: e.activation(DF[k2], DF[k2], ACT.Exp), T["d", b])
                    T["p", b] = pe.do(lambda e: e.transpose(banks[:, 3, P:P + 64], DF[k2], ident[0:64, 0:64]), x, get(("a", b - 1)))
                    T["a", b] = act.do(lambda e: e.activation(A[k3][:, :, 0:H], banks[:, 3, P:P + 64].rearrange("p (c h) -> p c h", h=H), ACT.Copy),
                                       T["p", b], get(("sg", b * BC + BC - 1 - R3 * BC)), get(("sm", b * BC + BC - 1 - R3 * BC)), get(("sb", b - R3)))

                def shared():
                    T["sb", b] = dve.do(lambda e: e.tensor_tensor(
                        SB[k3], A[k3][:, 1:BC:2, :], BND[:, b * BC // 2 + 1:(b + 1) * BC // 2 + 1].unsqueeze(2).broadcast_to([P, BC // 2, H + 1]), ALU.mult),
                        T["a", b], T["aw", b], get(("free", (b - R3) * BC + BC - 1)))

                return [exchange, maxima, expo, shared]

            def copy_sums(p):
                pv = banks[:, 4 + p % 2, 0:(H + 1) * WIN].rearrange("p (h w) -> p h w", w=WIN)
                ps = banks[0:H + 1, 6 + p % 2, 0:WIN]
                T["acc", p] = act.do(lambda e: e.activation(window(act, ACC, p), pv, ACT.Copy), T["sums", p], get(("acc", p - 1)), zero)
                T["sacc", p] = act.do(lambda e: e.activation(window(act, SACC, p), ps, ACT.Copy), get(("sacc", p - 1)))

            def chunk(b, j):
                c = b * BC + j
                p, even = c // 2, c % 2 == 0
                k4, k3, ks = b % R4, b % R3, c % RS
                pv = banks[:, 4 + p % 2, 0:(H + 1) * WIN]
                ps = banks[0:H + 1, 6 + p % 2, 0:WIN]

                def op():
                    if j == 0:
                        firsts(act, p, BC // 2)
                    T["sg", c] = dve.do(lambda e: e.tensor_tensor(
                        S[ks], OH[k4][:, j, :].unsqueeze(1).broadcast_to([P, H + 1, WIN]),
                        A[k3][:, j, :].unsqueeze(2).broadcast_to([P, H + 1, WIN]), ALU.mult),
                        T["a", b], T["aw", b], T["oh", b], get(("mm", c - RS)))
                    sv = S[ks].rearrange("p h w -> p (h w)")
                    g = G[:, c % RING, :]
                    if i == 0:
                        T["mm", c] = pe.do(lambda e: e.matmul(pv, g[:, 0:D], sv, start=even, stop=not even, skip_group_check=True),
                                           T["sg", c], T["g", c], get(("acc", p - 2)))
                    else:
                        pe.quiet(lambda e: e.matmul(pv[:, 0:H * WIN], g[:, 0:D], sv[:, 0:H * WIN], start=even, stop=not even, skip_group_check=True),
                                 T["sg", c], T["g", c], get(("acc", p - 2)))
                        T["mm", c] = pe.do(lambda e: e.matmul(pv[:, H * WIN:], g[:, D + H:], sv[:, H * WIN:], start=False, stop=not even, skip_group_check=True))
                    T["sm", c] = pe.do(lambda e: e.matmul(ps, A[k3][:, j, :], OH[k4][:, j, :], start=even, stop=not even, skip_group_check=True), get(("sacc", p - 2)))
                    if even:
                        T["free", c] = T["mm", c]
                    else:
                        T["sums", p] = T["sm", c]
                        copy_sums(p)
                    if even and p:
                        bb = (c - 1) // BC
                        sb = SB[bb % R3][:, (p - 1) % (BC // 2), :]
                        gb = G[:, (c - 1) % RING, :]
                        first = pv.rearrange("p (h w) -> p h w", w=WIN)[:, :, 0]
                        if i == 0:
                            pe.quiet(lambda e: e.matmul(first, gb[:, 0:D], sb, start=False, stop=False, skip_group_check=True), T["sb", bb])
                        else:
                            pe.quiet(lambda e: e.matmul(first[:, 0:H], gb[:, 0:D], sb[:, 0:H], start=False, stop=False, skip_group_check=True), T["sb", bb])
                            pe.quiet(lambda e: e.matmul(first[:, H:], gb[:, D + H:], sb[:, H:], start=False, stop=False, skip_group_check=True))
                        T["free", c - 1] = pe.do(lambda e: e.matmul(ps[:, 0:1], sb, ones[:, 0:1], start=False, stop=False, skip_group_check=True))
                    if j == BC - 1:
                        release(act)
                return op

            for p in range(NBATCH + 2):
                if p < NBATCH:
                    rows_of(p)
                    gathers(p)
                steps = []
                if 1 <= p <= NBATCH:
                    steps2 = s2(p - 1)
                else:
                    steps2 = []
                steps1 = s1(p) if p < NBATCH else []
                steps = steps1 + steps2
                main = [chunk(p - 2, j) for j in range(BC)] if p >= 2 else []
                for j in range(max(len(steps), len(main))):
                    if j < len(main):
                        main[j]()
                    if j < len(steps):
                        steps[j]()
            barrier()

        def weight_sums(space, SV):
            for b in range(NB):
                m = pe.do(lambda e, b=b: e.transpose(banks[:, 0, b * (H + 1):(b + 1) * (H + 1)], SACC[:, b * P:(b + 1) * P], ident[0:H + 1, 0:H + 1]))
            dve.do(lambda e: e.tensor_scalar_max(SV, banks[:, 0, 0:NB * (H + 1)].rearrange("p (b h) -> p b h", h=H + 1), 1e-16), m)
            return dve.chain(lambda e: e.reciprocal(SV, SV))

        def layer2_nodes0():
            K = D // H
            space = Space(node_at)
            SV = space.get([NB, H + 1])
            Wg, Wc = space.get([H, K]), space.get([D])
            ld2.dma(sp, lambda e: e.dma_start(Wg, gat[0]["W"].rearrange("h f k -> f h k")))
            w = ld2.dma(sp, lambda e: e.dma_start(Wc, a["L2_gnn_gcn_W0"]))
            weight_sums(space, SV)
            bfree = {}
            for g, (b0, n) in enumerate(groups()):
                k = g % 2
                for q in range(n):
                    b = b0 + q
                    for h in range(H):
                        pe.quiet(lambda e, b=b, q=q, h=h, k=k: e.matmul(
                            banks[:, 2 + k, q * D + h * K:q * D + (h + 1) * K], ACC[:, h, b * P:(b + 1) * P], Wg[:, h, :], start=True, stop=True), w, bfree.get(g - 2))
                    m = pe.do(lambda e, b=b, q=q, k=k: e.matmul(banks[:, 4 + k, q * D:(q + 1) * D], ACC[:, H, b * P:(b + 1) * P], Wc, start=True, stop=True))
                dve.do(lambda e, b0=b0, n=n, k=k: e.tensor_tensor(
                    X1[:, b0:b0 + n, :].rearrange("p b (h k) -> p b h k", h=H), banks[:, 2 + k, 0:n * D].rearrange("p (b h k) -> p b h k", h=H, k=K),
                    SV[:, b0:b0 + n, 0:H].unsqueeze(3).broadcast_to([P, n, H, K]), ALU.mult), m, dve.last())
                bfree[g] = dve.do(lambda e, b0=b0, n=n, k=k: e.tensor_tensor(
                    X2[:, b0:b0 + n, :], banks[:, 4 + k, 0:n * D].rearrange("p (b f) -> p b f", f=D),
                    SV[:, b0:b0 + n, H:H + 1].broadcast_to([P, n, D]), ALU.mult))
            EX = space.get([NB, D])
            dve.chain(lambda e: e.tensor_scalar_max(X2, X2, 0.0))
            t = dve.do(lambda e: e.tensor_scalar_min(EX, X1, 0.0))
            t = act.do(lambda e: e.activation(EX, EX, ACT.Exp), t)
            dve.do(lambda e: e.tensor_scalar_add(EX, EX, -1.0), t)
            dve.chain(lambda e: e.scalar_tensor_tensor(X1, X1, 0.0, EX, ALU.max, ALU.add))
            barrier()
            V = at(node_at, [2 * H])
            ES = at(node_at + 2 * H, [NB, 2 * H])
            done = scores(1, X1, V, ES, Space(node_at + 2 * H * (NB + 1)))
            st.dma(sp, lambda e: e.dma_start(blocks(gat1_table)[:, :, 0:D], X1), done)
            st.dma(sp, lambda e: e.dma_start(blocks(gat1_table)[:, :, D:D + H], ES[:, :, 0:H]))
            st.dma(sp, lambda e: e.dma_start(blocks(gat1_table)[:, :, D + H:], X2))
            st.dma(sp, lambda e: e.dma_start(blocks(ed_table[1]), ES[:, :, H:2 * H]))
            barrier()

        def layer2_nodes1():
            space = Space(node_at)
            SV = space.get([NB, H + 1])
            Wg, Wc = space.get([H, D]), space.get([D])
            PR = [space.get([H, D]) for _ in range(2)]
            C2 = space.get([NB, D])
            ld2.dma(sp, lambda e: e.dma_start(Wg, gat[1]["W"].rearrange("h f k -> f h k")))
            w = ld2.dma(sp, lambda e: e.dma_start(Wc, a["L2_gnn_gcn_W1"]))
            xr = ld.dma(sp, lambda e: e.dma_start(X1, blocks(x_rows)))
            weight_sums(space, SV)
            dve.chain(lambda e: e.tensor_scalar_mul(SV[:, :, 0:H], SV[:, :, 0:H], 1.0 / H))
            bfree = {}
            for b in range(NB):
                k = b % 2
                for h in range(H):
                    pe.quiet(lambda e, b=b, h=h, k=k: e.matmul(
                        banks[:, 2 + 2 * k + h // 4, (h % 4) * D:(h % 4 + 1) * D], ACC[:, h, b * P:(b + 1) * P], Wg[:, h, :], start=True, stop=True), w, bfree.get(b - 2))
                m = pe.do(lambda e, b=b, k=k: e.matmul(banks[:, 6 + k, 0:D], ACC[:, H, b * P:(b + 1) * P], Wc, start=True, stop=True))
                dve.do(lambda e, b=b, k=k: e.tensor_tensor(
                    PR[k], banks[:, 2 + 2 * k:4 + 2 * k, :].rearrange("p a (h f) -> p (a h) f", f=D),
                    SV[:, b, 0:H].unsqueeze(2).broadcast_to([P, H, D]), ALU.mult), m, dve.last())
                bfree[b] = dve.do(lambda e, b=b, k=k: e.tensor_scalar(C2[:, b, :], banks[:, 6 + k, 0:D], SV[:, b, H:H + 1], 0.0, ALU.mult, ALU.max))
                dve.do(lambda e, b=b, k=k: e.tensor_reduce(X2[:, b, :], PR[k].rearrange("p h f -> p f h"), AX_X, ALU.add), dve.last())
            dve.chain(lambda e: e.tensor_tensor(X2, X2, C2, ALU.max))
            dve.chain(lambda e: e.tensor_tensor(X1, X1, X2, ALU.add), xr)
            layer_norm(X1, X2, Space(node_at + NB * (H + 1)))
            st.dma(sp, lambda e: e.dma_start(blocks(x_rows), X1), dve.last())
            st.dma(sp, lambda e: e.dma_start(blocks(h_rows), X2))
            barrier()


        def layer3(diffusion):
            restored = landing("adj_restored")
            c_ready = restored.dma(act, lambda e: e.dma_start(CF, adj_rows)) if diffusion is None else None
            space = Space(tables_at)
            UU = [space.get([NB, 3 * D], BF16) for _ in range(2)]
            TB = space.get([STEPS, D])
            dinv, dinv2 = space.get([NB]), space.get([NB])
            R = 3
            HB = [space.get([D]) for _ in range(R)]
            TX = [space.get([D]) for _ in range(R)]
            UF = [space.get([D]) for _ in range(2)]
            R1 = [space.get([D]) for _ in range(2)]
            tn, tm = space.get([STEPS]), space.get([2])
            tr = ld2.dma(sp, lambda e: e.dma_start(tn, a["L3_gnn_t"].rearrange("k f -> f k")))
            dve.do(lambda e: e.tensor_reduce(tm[:, 0:1], tn, AX_X, ALU.max), tr)
            x = dve.chain(lambda e: e.tensor_scalar(tn, tn, tm[:, 0:1], None, ALU.subtract))
            x = act.do(lambda e: e.activation(tn, tn, ACT.Exp), x)
            dve.do(lambda e: e.tensor_reduce(tm[:, 1:2], tn, AX_X, ALU.add), x)
            dve.chain(lambda e: e.reciprocal(tm[:, 1:2], tm[:, 1:2]))
            x = dve.chain(lambda e: e.tensor_scalar(tn, tn, tm[:, 1:2], None, ALU.mult))
            for k in range(STEPS):
                m = pe.do(lambda e, k=k: e.matmul(banks[:, 1 + k // 4, (k % 4) * D:(k % 4 + 1) * D], tn[:, k:k + 1].broadcast_to([P, P]), ident, start=True, stop=True), x)
            dve.do(lambda e: e.tensor_copy(TB.rearrange("p k f -> p (k f)"), banks[:, 1:4, :].rearrange("p a f -> p (a f)")[:, 0:STEPS * D]), m)
            Y = at(tables_at, [NB, D])
            T = {}
            get = T.get

            def windows():
                for db in range(NB):
                    for sb in range(NB):
                        m = pe.do(lambda e, db=db, sb=sb: e.matmul(banks[:, 0, db:db + 1], C[:, sb, db * P:(db + 1) * P], onesb[:, 0:1],
                                                                   start=(sb == 0), stop=(sb == NB - 1), skip_group_check=True), c_ready)
                dve.chain(lambda e: e.tensor_scalar_add(dinv2, banks[:, 0, 0:NB], 1.0), m)
                x = act.do(lambda e: e.activation(dinv, dinv2, ACT.Sqrt), dve.last())
                dve.do(lambda e: e.reciprocal(dinv, dinv), x)
                dve.do(lambda e: e.reciprocal(dinv2, dinv2), dve.last())
                scales = dve.last()

                hb = [landing(f"hb{k}") for k in range(R)]
                n = 0
                for k in range(STEPS - 1, -1, -1):
                    new, old = UU[k % 2], UU[(k + 1) % 2]
                    for db in range(NB):
                        r, r2, bk = n % R, n % 2, n % 6
                        T["hb", n] = hb[r].dma(sp, lambda e, r=r, db=db: e.dma_start(HB[r], h_rows[db * P:(db + 1) * P, :]), get(("t", n - R)))
                        T["t", n] = pool.do(lambda e, r=r, k=k: e.tensor_tensor(TX[r], HB[r], TB[:, k, :], ALU.mult), T["hb", n], scales, get(("u", n - R)))
                        if k:
                            T["tx", n] = pool.do(lambda e, r=r, db=db: e.tensor_scalar(TX[r], TX[r], dinv[:, db:db + 1], None, ALU.mult), T["t", n])
                        else:
                            T["tx", n] = T["t", n]
                        if k < STEPS - 1:
                            acc = banks[:, bk, 0:3 * D]
                            pe.quiet(lambda e, acc=acc, old=old, db=db: e.matmul(acc, identb, old[:, db, :], start=True, stop=False),
                                     T["split", n - NB - db + NB - 1], get(("red", n - 6)), scales)
                            for sb in range(NB):
                                f = lambda e, acc=acc, old=old, db=db, sb=sb: e.matmul(acc, C[:, sb, db * P:(db + 1) * P], old[:, sb, :], start=False, stop=(sb == NB - 1))
                                if sb < NB - 1:
                                    pe.quiet(f)
                            T["mm", n] = pe.do(f)
                            T["red", n] = dve.do(lambda e, acc=acc, r2=r2: e.tensor_reduce(
                                UF[r2], acc.rearrange("p (j f) -> p f j", j=3), AX_X, ALU.add), T["mm", n], get(("split", n - 2)))
                            if k:
                                T["u", n] = dve.chain(lambda e, r=r, r2=r2, db=db: e.scalar_tensor_tensor(UF[r2], UF[r2], dinv2[:, db:db + 1], TX[r], ALU.mult, ALU.add), T["tx", n])
                            else:
                                T["u", n] = T["split", n] = dve.chain(lambda e, r=r, r2=r2, db=db: e.scalar_tensor_tensor(
                                    Y[:, db, :], UF[r2], dinv[:, db:db + 1], TX[r], ALU.mult, ALU.add), T["tx", n])
                        else:
                            T["u", n] = dve.do(lambda e, r=r, r2=r2: e.tensor_copy(UF[r2], TX[r]), T["tx", n], get(("split", n - 2)))
                        if k:
                            part = [new[:, db, j * D:(j + 1) * D] for j in range(3)]
                            T["hi", n] = act.do(lambda e, r2=r2, part=part: e.activation(part[0], UF[r2], ACT.Copy), T["u", n], get(("mm", n - db - 1)))
                            dve.do(lambda e, r2=r2, part=part: e.tensor_tensor(R1[r2], UF[r2], part[0], ALU.subtract), T["hi", n])
                            dve.chain(lambda e, r2=r2, part=part: e.tensor_copy(part[1], R1[r2]))
                            T["split", n] = dve.chain(lambda e, r2=r2, part=part: e.tensor_tensor(part[2], R1[r2], part[1], ALU.subtract))
                        n += 1

            if diffusion is None:
                windows()
            else:
                diffusion(TB, Y)
            barrier()
            space = Space(tables_at + NB * 3 * D)
            Wi, Wr, Bi = (space.get([D]) for _ in range(3))
            Xr = [space.get([4, D]) for _ in range(2)]
            YT = [at(tables_at + NB * 3 * D // 2 + k * 4 * D, [4 * D]) for k in range(2)]
            XO = [at(tables_at + NB * 3 * D // 2 + (2 + k) * 4 * D, [4, D]) for k in range(2)]
            ld2.dma(sp, lambda e: e.dma_start(Wi, a["L3_gnn_init_weight"][0]))
            ld2.dma(sp, lambda e: e.dma_start(Wr, a["L3_gnn_root_weight"][0, 0]))
            w = load_row(ld2, Bi, a["L3_gnn_bias"][0, 0, 0])
            xl = [landing(f"xl{k}") for k in range(2)]
            ol = [landing(f"ol{k}") for k in range(2)]
            for g, (b0, n) in enumerate(groups()):
                k = g % 2
                T["x", g] = xl[k].dma(sp, lambda e, k=k, b0=b0, n=n: e.dma_start(Xr[k][:, 0:n, :], blocks(x_rows)[:, b0:b0 + n, :]), get(("o", g - 2)))
                for q in range(n):
                    m = pe.do(lambda e, q=q, k=k, b0=b0: e.transpose(banks[:, k, q * P:(q + 1) * P], Y[:, b0 + q, :], ident), get(("yt", g - 2)))
                T["yt", g] = act.do(lambda e, k=k, n=n: e.activation(YT[k][:, 0:n * P], banks[:, k, 0:n * P], ACT.Copy), m, get(("mo", g - 2)))
                for q in range(n):
                    ov = banks[:, 2 + k, q * D:(q + 1) * D]
                    pe.quiet(lambda e, q=q, k=k, ov=ov: e.matmul(ov, YT[k][:, q * P:(q + 1) * P], Wi, start=True, stop=False), T["yt", g], w, get(("b", g - 2)))
                    T["mo", g] = pe.do(lambda e, q=q, k=k, ov=ov: e.matmul(ov, YT[k][:, q * P:(q + 1) * P], Wr, start=False, stop=True))
                xo = XO[k][:, 0:n, :]
                T["b", g] = dve.do(lambda e, k=k, n=n, xo=xo: e.tensor_tensor(
                    xo, banks[:, 2 + k, 0:n * D].rearrange("p (b f) -> p b f", f=D), Bi.unsqueeze(1).broadcast_to([P, n, D]), ALU.add), T["mo", g], w, get(("s", g - 2)))
                T["o", g] = dve.chain(lambda e, k=k, n=n, xo=xo: e.scalar_tensor_tensor(xo, xo, 0.0, Xr[k][:, 0:n, :], ALU.max, ALU.add), T["x", g])
                if b0 + n < NB:
                    T["s", g] = ol[k].dma(act, lambda e, b0=b0, n=n, xo=xo: e.dma_start(blocks(out[b0 * P:(b0 + n) * P, :]), xo), T["o", g])
                else:
                    r = N - b0 * P
                    T["s", g] = ol[k].dma(act, lambda e, b0=b0, r=r, xo=xo: e.dma_start(out[b0 * P:N, :], xo[0:r, 0, :]), T["o", g])


        low = Space(ring_at + 2 * NP, CW)
        KI, GI, DI = (low.get([1], I32) for _ in range(3))
        WV, KF, DUMP, CNT, MARK = (low.get([1]) for _ in range(5))
        EQ, TRI, PR = (low.get([P]) for _ in range(3))
        GR = low.get([2 * D + H])
        EDG, ZG, MG = (low.get([H]) for _ in range(3))
        COLS = (H + 1) * D + H + 1
        V, CUR = low.get([COLS]), low.get([COLS])
        t_sum = [dram(f"any_sums{i}", [NP + P, D + 1]) for i in range(2)]
        t_att = [dram(f"any_attention{i}", [NP + P, COLS]) for i in range(2)]
        t_max = [dram(f"any_maxima{i}", [NP + P, H]) for i in range(2)]
        t_dif = dram("any_diffusion", [NP + P, D])
        t_src = dram("any_sources", [NP, D])

        def serial(fill):
            barrier()
            s = Serial(turn_sems, pool_landed)
            s.step(dve, lambda e, i: e.memset(MARK, 0.0))
            fill(s)
            s.step(dve, lambda e, i: e.memset(MARK, 0.0))
            s.close(dve)
            dve.do(lambda e: e.memset(MARK, 0.0))
            barrier()

        def setup_any(s):
            s.step(pool, lambda e, i: e.memset(TRI, 1.0))
            s.step(pool, lambda e, i: e.affine_select(out=TRI, in_=TRI, compare_op=ALU.is_ge, fill=0.0, base=-1,
                                                      pattern=[[-1, P]], channel_multiplier=1))
            s.step(pool, lambda e, i: e.iota(DI, [[0, 1]], base=NP, channel_multiplier=1))
            s.step(dve, lambda e, i: e.tensor_copy(DUMP, DI))

        def fill_table(s, table, value, cols):
            n = table.shape[0] // P
            s.step(dve, lambda e, i: e.memset(V[:, 0:cols], value))
            s.step(sp, lambda e, i: e.dma_start(table.rearrange("(b p) f -> p b f", p=P), V[:, 0:cols].unsqueeze(1).broadcast_to([P, n, cols])))

        def scatter(s, table, cols, key, other, values, biggest=False):
            def rows(dst, src, index):
                return lambda e, i: e.indirect_dma_start(dst, None, src, bass.IndirectOffsetOnAxis(ap=index.bitcast(U32), axis=0))

            def fill():
                part = lambda v, i: v[0:1, bass.ds(i * P + 1, P)].rearrange("o p -> p o")
                s.step(dve, lambda e, i: e.memset(MARK, 0.0))
                s.step(sp, lambda e, i: e.dma_start(KI, part(key, i)))
                s.step(sp, lambda e, i: e.dma_start(GI, part(other, i)))
                s.step(sp, lambda e, i: e.dma_start(WV, part(weight_flat, i)))
                s.step(dve, lambda e, i: e.tensor_copy(KF, KI))
                s.step(pe, lambda e, i: e.matmul(banks[:, 0, 0:P], KF.broadcast_to([P, P]), ident, start=True, stop=True))
                s.step(dve, lambda e, i: e.tensor_scalar(EQ, banks[:, 0, 0:P], KF, None, ALU.is_equal))
                s.step(dve, lambda e, i: e.tensor_tensor(PR, EQ, TRI, ALU.mult))
                s.step(dve, lambda e, i: e.tensor_reduce(CNT, PR, AX_X, ALU.add))
                s.step(dve, lambda e, i: e.tensor_scalar(CNT, CNT, 0.0, None, ALU.is_equal))
                s.step(dve, lambda e, i: e.tensor_tensor(KF, KF, DUMP, ALU.subtract))
                s.step(dve, lambda e, i: e.tensor_tensor(KF, KF, CNT, ALU.mult))
                s.step(dve, lambda e, i: e.tensor_tensor(KF, KF, DUMP, ALU.add))
                s.step(dve, lambda e, i: e.tensor_copy(DI, KF))
                values(rows)
                s.pool_dma(pool, rows(CUR[:, 0:cols], table, KI))
                if biggest:
                    s.step(dve, lambda e, i: e.tensor_scalar(EQ, EQ, -1.0, BIG, ALU.add, ALU.mult))
                    for h in range(cols):
                        s.step(pe, lambda e, i, h=h: e.matmul(banks[:, 1, 0:P], V[:, h:h + 1].broadcast_to([P, P]), ident, start=True, stop=True))
                        s.step(dve, lambda e, i: e.tensor_tensor(PR, banks[:, 1, 0:P], EQ, ALU.add))
                        s.step(dve, lambda e, i: e.tensor_reduce(CNT, PR, AX_X, ALU.max))
                        s.step(dve, lambda e, i, h=h: e.tensor_tensor(CUR[:, h:h + 1], CUR[:, h:h + 1], CNT, ALU.max))
                else:
                    for b, c in enumerate(range(0, cols, 512)):
                        n = min(512, cols - c)
                        s.step(pe, lambda e, i, b=b, c=c, n=n: e.matmul(banks[:, 1 + b, 0:n], EQ, V[:, c:c + n], start=True, stop=True))
                        s.step(dve, lambda e, i, b=b, c=c, n=n: e.tensor_tensor(CUR[:, c:c + n], CUR[:, c:c + n], banks[:, 1 + b, 0:n], ALU.add))
                s.pool_dma(pool, lambda e, i: e.indirect_dma_start(table, bass.IndirectOffsetOnAxis(ap=DI.bitcast(U32), axis=0), CUR[:, 0:cols], None))
            s.loop(NC, fill)

        def any_sums(layer):
            key, other, rows_in, into = ((dst_flat, src_flat, h_table, ACC0), (src_flat, dst_flat, h_rows, AGG))[layer]
            LB = at(0, [D + 1])

            def go(s):
                if layer == 0:
                    setup_any(s)
                fill_table(s, t_sum[layer], 0.0, D + 1)

                def values(rows):
                    s.pool_dma(pool, rows(GR[:, 0:D], rows_in, GI))
                    if layer == 0:
                        s.step(dve, lambda e, i: e.tensor_scalar(V[:, 0:D], GR[:, 0:D], WV, None, ALU.mult))
                    else:
                        s.step(dve, lambda e, i: e.tensor_copy(V[:, 0:D], GR[:, 0:D]))
                    s.step(dve, lambda e, i: e.memset(V[:, D:D + 1], 1.0))

                scatter(s, t_sum[layer], D + 1, key, other, values)
                s.step(dve, lambda e, i: e.memset(MARK, 0.0))
                for b in range(NB):
                    s.step(sp, lambda e, i, b=b: e.dma_start(LB, t_sum[layer][b * P:(b + 1) * P, :]))
                    s.step(pe, lambda e, i: e.transpose(banks[:, 0, 0:P], LB[:, 0:D], ident))
                    s.step(dve, lambda e, i, b=b: e.tensor_copy(into[:, b * P:(b + 1) * P], banks[:, 0, 0:P]))
                    if layer:
                        s.step(dve, lambda e, i, b=b: e.tensor_copy(odeg[:, b:b + 1], LB[:, D:D + 1]))
            serial(go)

        def any_attention(i2):
            table, row = (gat0_table, D + H) if i2 == 0 else (gat1_table, 2 * D + H)
            LB = at(ring_at, [COLS])

            def go(s):
                fill_table(s, t_max[i2], -BIG, H)
                fill_table(s, t_att[i2], 0.0, COLS)

                def logits(rows, out):
                    s.pool_dma(pool, rows(GR[:, 0:row], table, GI))
                    s.pool_dma(pool, rows(EDG, ed_table[i2], KI))
                    s.step(dve, lambda e, i: e.tensor_tensor(ZG, GR[:, D:D + H], EDG, ALU.add))
                    s.step(dve, lambda e, i: e.scalar_tensor_tensor(out, ZG, 0.2, ZG, ALU.mult, ALU.max))

                scatter(s, t_max[i2], H, dst_flat, src_flat, lambda rows: logits(rows, V[:, 0:H]), biggest=True)

                def values(rows):
                    logits(rows, EDG)
                    s.pool_dma(pool, rows(MG, t_max[i2], KI))
                    s.step(dve, lambda e, i: e.tensor_tensor(ZG, EDG, MG, ALU.subtract))
                    s.step(act, lambda e, i: e.activation(ZG, ZG, ACT.Exp))
                    s.step(dve, lambda e, i: e.tensor_tensor(
                        V[:, 0:H * D].rearrange("p (h f) -> p h f", f=D), GR[:, 0:D].unsqueeze(1).broadcast_to([P, H, D]),
                        ZG.unsqueeze(2).broadcast_to([P, H, D]), ALU.mult))
                    second = GR[:, 0:D] if i2 == 0 else GR[:, D + H:]
                    s.step(dve, lambda e, i: e.tensor_scalar(V[:, H * D:(H + 1) * D], second, WV, None, ALU.mult))
                    s.step(dve, lambda e, i: e.tensor_copy(V[:, (H + 1) * D:COLS - 1], ZG))
                    s.step(dve, lambda e, i: e.tensor_copy(V[:, COLS - 1:COLS], WV))

                scatter(s, t_att[i2], COLS, dst_flat, src_flat, values)
                s.step(dve, lambda e, i: e.memset(MARK, 0.0))
                for b in range(NB):
                    s.step(sp, lambda e, i, b=b: e.dma_start(LB, t_att[i2][b * P:(b + 1) * P, :]))
                    for h in range(H + 1):
                        s.step(pe, lambda e, i, h=h: e.transpose(banks[:, 0, 0:P], LB[:, h * D:(h + 1) * D], ident))
                        s.step(dve, lambda e, i, b=b, h=h: e.tensor_copy(ACC[:, h, b * P:(b + 1) * P], banks[:, 0, 0:P]))
                    s.step(pe, lambda e, i: e.transpose(banks[0:H + 1, 0, 0:P], LB[:, (H + 1) * D:COLS], ident))
                    s.step(dve, lambda e, i, b=b: e.tensor_copy(SACC[:, b * P:(b + 1) * P], banks[0:H + 1, 0, 0:P]))
            serial(go)

        def any_diffusion(TB, Y):
            space = Space(0, ring_at)
            HX, U, DG = space.get([NB, D]), space.get([NB, D]), space.get([NB])

            def go(s):
                s.step(sp, lambda e, i: e.dma_start(HX, blocks(h_rows)))
                s.step(sp, lambda e, i: e.dma_start(DG.unsqueeze(2), blocks(t_sum[0][0:NP, :])[:, :, D:D + 1]))
                s.step(dve, lambda e, i: e.tensor_scalar_add(DG, DG, 1.0))
                s.step(act, lambda e, i: e.activation(DG, DG, ACT.Sqrt))
                s.step(dve, lambda e, i: e.reciprocal(DG, DG))
                by_degree = DG.unsqueeze(2).broadcast_to([P, NB, D])
                s.step(dve, lambda e, i: e.tensor_tensor(Y, HX, TB[:, STEPS - 1, :].unsqueeze(1).broadcast_to([P, NB, D]), ALU.mult))
                for k in range(STEPS - 2, -1, -1):
                    s.step(dve, lambda e, i: e.tensor_tensor(U, Y, by_degree, ALU.mult))
                    s.step(sp, lambda e, i: e.dma_start(blocks(t_src), U))
                    s.step(sp, lambda e, i: e.dma_start(blocks(t_dif[0:NP, :]), U))
                    s.step(sp, lambda e, i: e.dma_start(t_dif[NP:NP + P, :], U[:, 0, :]))
                    scatter(s, t_dif, D, dst_flat, src_flat, lambda rows: s.pool_dma(pool, rows(V[:, 0:D], t_src, GI)))
                    s.step(dve, lambda e, i: e.memset(MARK, 0.0))
                    s.step(sp, lambda e, i: e.dma_start(U, blocks(t_dif[0:NP, :])))
                    s.step(dve, lambda e, i: e.tensor_tensor(U, U, by_degree, ALU.mult))
                    s.step(dve, lambda e, i, k=k: e.tensor_tensor(Y, HX, TB[:, k, :].unsqueeze(1).broadcast_to([P, NB, D]), ALU.mult))
                    s.step(dve, lambda e, i: e.tensor_tensor(Y, Y, U, ALU.add))
            serial(go)

        def regular():
            layer0_edges()
            layer0_nodes()
            layer1_sums()
            layer1_nodes()
            layer2_tables0()
            layer2_edges(0)
            layer2_nodes0()
            layer2_edges(1)
            layer2_nodes1()
            layer3(None)
            barrier()

        def any_edges():
            any_sums(0)
            layer0_nodes()
            any_sums(1)
            layer1_nodes()
            layer2_tables0()
            any_attention(0)
            layer2_nodes0()
            any_attention(1)
            layer2_nodes1()
            layer3(any_diffusion)
            barrier()

        counts, landed = snapshot()
        take(common)
        for name, program in (("regular", regular), ("any", any_edges)):
            for l in lanes:
                l.count, l.waited = counts[id(l)][0], dict(counts[id(l)][1])
            for x in landings:
                x.count = landed.get(id(x), 0)
            program()
            branches[name] = {}
            take(branches[name])
        finish()


_OUTS = [((N, D), "float32")]


def kernel(**inputs):
    import numpy as _np
    import concourse.bacc as _bacc
    from concourse import mybir as _mybir
    from concourse.bass_utils import run_bass_kernel_spmd as _run

    nc = _bacc.Bacc("TRN2", target_bir_lowering=False, num_devices=1)
    arrays, args = {}, {}
    for name in inputs:
        v = _np.ascontiguousarray(inputs[name])
        arrays[f"in_{name}"] = v
        args[name] = nc.dram_tensor(f"in_{name}", v.shape, _mybir.dt.from_np(v.dtype), kind="ExternalInput").ap()
    out = nc.dram_tensor("out", [N, D], F32, kind="ExternalOutput").ap()
    build(nc, args, out)
    r = _run(nc, [arrays], core_ids=[0])
    return r.results[0]["out"]
```

```python
from contextlib import ExitStack

import concourse.bass as bass
from concourse import mybir

F32, BF16 = mybir.dt.float32, mybir.dt.bfloat16
I32, U32, I16 = mybir.dt.int32, mybir.dt.uint32, mybir.dt.int16
ALU = mybir.AluOpType
ACT = mybir.ActivationFunctionType
AX_X = mybir.AxisListType.X

P = 128
D = 128
N = 3125
NB = -(-N // P)
NP = NB * P
E = 50000
NC = 392
WIN = 16
H = 8
BC = 8
NBATCH = NC // BC
BIG = 1e30
STEPS = 10
GUARD = 5000


class Lane:

    def __init__(self, sem):
        self.sem, self.count, self.ops, self.waited = sem, 0, [], {}

    def wait(self, *tokens):
        for token in tokens:
            if token is None:
                continue
            sem, value = token
            if self.waited.get(id(sem), 0) < value:
                self.waited[id(sem)] = value
                self.ops.append(lambda e, s=sem, v=value: e.wait_ge(s, v))

    def do(self, make, *waits):
        self.wait(*waits)
        self.count += 1
        self.ops.append(lambda e: make(e).then_inc(self.sem, 1))
        return (self.sem, self.count)

    def quiet(self, make, *waits):
        self.wait(*waits)
        self.ops.append(make)

    def last(self):
        return (self.sem, self.count)

    def chain(self, make, *waits):
        return self.do(make, self.last(), *waits)


class Landing:

    def __init__(self, sem):
        self.sem, self.count = sem, 0

    def dma(self, lane, make, *waits):
        lane.wait(*waits)
        self.count += 16
        lane.ops.append(lambda e: make(e).then_inc(self.sem, 16))
        return (self.sem, self.count)

    def last(self):
        return (self.sem, self.count) if self.count else None


class Serial:

    def __init__(self, turn_sems, landed):
        self.turns, self.landed, self.items = turn_sems, landed, []
        self.at = self.items

    def step(self, lane, make):
        self.at.append((lane, make, 0))

    def pool_dma(self, lane, make):
        self.at.append((lane, make, 1))

    def loop(self, count, fill):
        outer, body = self.at, []
        self.at = body
        fill()
        self.at = outer
        outer.append((count, body))

    @staticmethod
    def head(items):
        return Serial.head(items[0][1]) if len(items[0]) == 2 else items[0][0]

    def lanes_of(self, items):
        return {y for x in items for y in (self.lanes_of(x[1]) if len(x) == 2 else {x[0]})}

    def emit(self, items, after, put):
        for k, item in enumerate(items):
            nxt = self.head(items[k + 1:]) if k + 1 < len(items) else after
            if len(item) == 2:
                count, body = item
                assert self.head(body) is nxt
                inner = {}
                self.emit(body, nxt, lambda lane, op: inner.setdefault(id(lane), []).append(op))
                for lane in self.lanes_of(body):
                    def run(e, i, count=count, ops=inner[id(lane)]):
                        with e.Fori(0, count) as j:
                            for op in ops:
                                op(e, j)
                    put(lane, run)
            else:
                lane, make, by_pool_dma = item
                turn, give = self.turns[id(lane)], self.turns[id(nxt)]

                def run(e, i, make=make, turn=turn, give=give, landed=self.landed if by_pool_dma else None):
                    e.wait_ge(turn, 16)
                    e.sem_clear(turn)
                    if landed is None:
                        make(e, i).then_inc(give, 16)
                    else:
                        make(e, i).then_inc(landed, 16)
                        e.wait_ge(landed, 16)
                        e.dma_reset(range(landed.num, landed.num + 1))
                        e.sem_clear(landed)
                        e.sem_inc(give, 16)
                put(lane, run)

    def close(self, lane):
        assert self.head(self.items) is lane
        turn = self.turns[id(lane)]
        lane.ops.append(lambda e: e.sem_inc(turn, 16))
        self.emit(self.items, lane, lambda l, op: l.ops.append(lambda e: op(e, None)))
        lane.ops.append(lambda e: e.wait_ge(turn, 16))
        lane.ops.append(lambda e: e.sem_clear(turn))


def build(nc, a, out, *_):
    ctx = ExitStack()
    with ctx:
        sem = lambda name: ctx.enter_context(nc.semaphore(name))
        WORDS = 53200
        CW = NB * NP // 2
        arena = ctx.enter_context(nc.sbuf_tensor("arena", [P, WORDS], F32))
        banks = ctx.enter_context(nc.psum_tensor("banks", [P, 8, 512], F32))

        def at(word, shape, dt=F32, parts=P):
            n = 1
            for s in shape:
                n *= s
            w = n if dt in (F32, I32, U32) else -(-n // 2)
            assert word + w <= WORDS, (word, w)
            v = arena[0:parts, word:word + w]
            if dt != F32:
                v = v.bitcast(dt)
            if len(shape) == 2:
                v = v.rearrange("p (a b) -> p a b", b=shape[1])
            if len(shape) == 3:
                v = v.rearrange("p (a b c) -> p a b c", b=shape[1], c=shape[2])
            return v

        class Space:

            def __init__(self, word, end=WORDS):
                self.word, self.end = word, end

            def get(self, shape, dt=F32, parts=P):
                n = 1
                for s in shape:
                    n *= s
                v = at(self.word, shape, dt, parts)
                self.word += n if dt in (F32, I32, U32) else -(-n // 2)
                assert self.word <= self.end, "the arena is full"
                return v

        sp, act, pool = Lane(sem("sp")), Lane(sem("act")), Lane(sem("pool"))
        dve, pe = Lane(sem("dve")), Lane(sem("pe"))
        lanes = [sp, act, pool, dve, pe]
        turn_sems = {id(l): sem(f"turn_{n}") for n, l in zip(("sp", "act", "pool", "dve", "pe"), lanes)}
        pool_landed = sem("pool_landed")
        ctx.enter_context(nc.allow_non_contiguous_dma(reason="columns of single words, in small numbers"))
        landings = []

        named = {}

        def landing(name):
            if name not in named:
                named[name] = Landing(sem(name))
                landings.append(named[name])
            return named[name]

        def barrier():
            for lane in lanes:
                for other in lanes:
                    if other.count:
                        lane.wait(other.last())
                for x in landings:
                    lane.wait(x.last())

        def dram(name, shape, dt=F32):
            return nc.dram_tensor(name, shape, dt).ap()

        h_table = dram("h_table", [NP, D])
        x_rows = dram("x_rows", [NP, D])
        h_rows = dram("h_rows", [NP, D])
        gat0_table = dram("gat0_table", [NP, D + H])
        gat1_table = dram("gat1_table", [NP, 2 * D + H])
        ed_table = [dram(f"ed_table{i}", [NP, H]) for i in range(2)]
        adj_rows = dram("adj_rows", [P, CW])
        dst_flat = dram("dst_flat", [1, NC * P + 2], I32)
        src_flat = dram("src_flat", [1, NC * P + 2], I32)
        weight_flat = dram("weight_flat", [1, NC * P + 2])

        def blocks(ap):
            return ap.rearrange("(b p) f -> p b f", p=P)

        common, branches = {}, {}

        def snapshot():
            return ({id(l): (l.count, dict(l.waited)) for l in lanes}, {id(x): x.count for x in landings})

        def take(into):
            for l in lanes:
                into[id(l)] = l.ops
                l.ops = []

        def finish():
            with nc.Block() as block:
                for deco, lane in ((block.sync, sp), (block.scalar, act), (block.gpsimd, pool), (block.vector, dve), (block.tensor, pe)):
                    def body(e, lane=lane):
                        for op in common[id(lane)]:
                            op(e)
                        spread = e.alloc_register("spread")
                        e.reg_load(spread, FLAG[0:1, 0:1])
                        with e.If_eq(spread, 0):
                            for op in branches["regular"][id(lane)]:
                                op(e)
                        with e.Else():
                            for op in branches["any"][id(lane)]:
                                op(e)
                    deco(body)

        keep = Space(CW)
        wide = keep.get([3 * P])
        ident = wide[:, P:2 * P]
        identb = keep.get([P], BF16)
        ones = keep.get([P])
        onesb = keep.get([2], BF16)
        iota_w = keep.get([WIN])
        win_row = keep.get([1])
        slot_mask = keep.get([BC])
        tables_at = keep.word
        SRC = keep.get([NC], I32)
        REL = keep.get([NC])
        WT = keep.get([NC])
        FI = keep.get([NC], I32)
        SHARED = keep.get([NC])
        EDI = keep.get([NBATCH], I32)
        FLAG = keep.get([1], I32)
        keep_end = keep.word
        C = at(0, [NB, NP], BF16)
        CF = at(0, [CW])
        ACC0 = at(keep_end, [NP])
        AGG = at(keep_end, [NP])
        odeg = at(keep_end + NP + NB * 3 * D // 2, [NB])

        ld = landing("ld")
        ld2 = landing("ld2")
        st = landing("st")

        tmpi = Space(keep_end)
        ti = tmpi.get([WIN], I32)
        tq = tmpi.get([1], I32)
        tp = tmpi.get([1], I32)
        tpf = tmpi.get([1])
        pool.do(lambda e: e.memset(wide, 0.0))
        pool.chain(lambda e: e.affine_select(out=wide, in_=wide, compare_op=ALU.not_equal, fill=1.0, base=P,
                                             pattern=[[-1, 3 * P]], channel_multiplier=1))
        pool.do(lambda e: e.memset(ones, 1.0))
        pool.do(lambda e: e.memset(onesb, 1.0))
        pool.do(lambda e: e.iota(ti, [[1, WIN]], base=0, channel_multiplier=0))
        pool.do(lambda e: e.iota(tq, [[0, 1]], base=0, channel_multiplier=1))
        pool.do(lambda e: e.iota(tp, [[0, 1]], base=0, channel_multiplier=1))
        c0 = pool.last()
        dve.do(lambda e: e.tensor_copy(identb, ident), c0)
        dve.do(lambda e: e.tensor_copy(iota_w, ti))
        dve.chain(lambda e: e.tensor_single_scalar(tq, tq, BC - 1, ALU.bitwise_and))
        dve.chain(lambda e: e.tensor_copy(win_row, tq))
        dve.chain(lambda e: e.tensor_copy(tpf, tp))
        dve.chain(lambda e: e.tensor_scalar(slot_mask, iota_w[:, 0:BC], win_row, None, ALU.is_equal))
        dve.chain(lambda e: e.tensor_tensor(win_row, tpf, win_row, ALU.subtract))
        dve.chain(lambda e: e.tensor_scalar_mul(win_row, win_row, 1.0 / BC))

        T = NC // P + 1
        s0 = Space(tmpi.word)
        raw = {k: s0.get([T, P], F32 if k == "w" else I32) for k in "sdw"}
        sf, df, rf = s0.get([T, P]), s0.get([T, P]), s0.get([T, P])
        FB = s0.get([NC])
        fills = {"s": N, "d": N, "w": 0.0}
        full = E // P
        for k in "sdw":
            pool.do(lambda e, v=raw[k][:, T - 1, :], x=fills[k]: e.memset(v, x))
        srcs = {"s": a["src"], "d": a["dst"], "w": a["edge_weight"]}
        tok = []
        for i, k in enumerate("sdw"):
            z = landing(f"edges_{k}")
            v = srcs[k]
            body = v[0:(T - 1) * P * P].rearrange("(t p e) -> p t e", p=P, e=P)
            rest = v[(T - 1) * P * P:full * P].rearrange("(p e) -> p e", e=P)
            tail = v[full * P:E].rearrange("(p e) -> p e", p=1)
            nf = full - (T - 1) * P
            z.dma(sp, lambda e, b=body, k=k: e.dma_start(raw[k][:, 0:T - 1, :], b), pool.last())
            z.dma(sp, lambda e, b=rest, k=k, nf=nf: e.dma_start(raw[k][0:nf, T - 1, :], b))
            tok.append(z.dma(sp, lambda e, b=tail, k=k, nf=nf: e.dma_start(raw[k][nf:nf + 1, T - 1, 0:E - full * P], b)))
        dve.do(lambda e: e.tensor_copy(sf, raw["s"]), tok[0])
        dve.do(lambda e: e.tensor_copy(df, raw["d"]), tok[1])
        for t in range(T):
            dve.do(lambda e, t=t: e.tensor_scalar(rf[:, t, :], df[:, t, :], df[:, t, 0:1], None, ALU.subtract), dve.last())
        tabs = dve.last()
        gtile = s0.get([2], I32)
        pool.do(lambda e: e.memset(gtile, GUARD))
        nr = NC - (T - 1) * P
        for i, (k, table) in enumerate((("s", src_flat), ("d", dst_flat), ("w", weight_flat))):
            flat = table[0:1, :]
            guard = gtile[0:1, 0:1] if k != "w" else gtile[0:1, 0:1].bitcast(F32)
            st.dma(sp, lambda e, k=k, flat=flat: e.dma_start(flat[:, 1:1 + (T - 1) * P * P].rearrange("o (t p e) -> (o p) t e", p=P, e=P), raw[k][:, 0:T - 1, :]), tok[i], pool.last())
            st.dma(sp, lambda e, k=k, flat=flat: e.dma_start(flat[:, 1 + (T - 1) * P * P:1 + NC * P].rearrange("o (p e) -> (o p) e", e=P), raw[k][0:nr, T - 1, :]))
            st.dma(sp, lambda e, flat=flat, guard=guard: e.dma_start(flat[:, 0:1], guard))
            st.dma(sp, lambda e, flat=flat, guard=guard: e.dma_start(flat[:, NC * P + 1:NC * P + 2], guard))
        prev = {}
        for i, (v, o) in enumerate(((sf, SRC), (rf, REL), (raw["w"], WT))):
            for t in range(T):
                n = min(P, NC - t * P)
                bk = (i * T + t) % 4
                tr = pe.do(lambda e, v=v, t=t, n=n, bk=bk: e.transpose(banks[:, bk, 0:n], v[0:n, t, :], ident[0:n, 0:n]),
                           tabs, tok[2], c0, prev.get(bk))
                prev[bk] = dve.do(lambda e, o=o, t=t, n=n, bk=bk: e.tensor_copy(o[:, t * P:t * P + n], banks[:, bk, 0:n]), tr)
        for t in range(T):
            n = min(P, NC - t * P)
            tr = pe.do(lambda e, t=t, n=n: e.matmul(banks[:, 4, t * P:t * P + n], df[0:n, t, 0:1].broadcast_to([n, P]),
                                                    ident[0:n, 0:n], start=True, stop=True))
        dve.do(lambda e: e.tensor_copy(FB, banks[:, 4, 0:NC]), tr)
        dve.chain(lambda e: e.tensor_copy(FI, FB))
        picked = s0.get([NBATCH, BC])
        ed_row = s0.get([NBATCH])
        dve.do(lambda e: e.tensor_tensor(picked, FB.rearrange("p (b j) -> p b j", j=BC), slot_mask.unsqueeze(1).broadcast_to([P, NBATCH, BC]), ALU.mult))
        dve.chain(lambda e: e.tensor_reduce(ed_row, picked, AX_X, ALU.add))
        dve.chain(lambda e: e.tensor_scalar(EDI, ed_row, win_row, None, ALU.add))
        bad = s0.get([8])
        cmp = s0.get([T, P])
        step = s0.get([NC])

        def count_of(k, v, make):
            dve.chain(make)
            dve.chain(lambda e, k=k, v=v: e.tensor_reduce(bad[:, k:k + 1], v, AX_X if len(v.shape) == 2 else mybir.AxisListType.XY, ALU.add))

        dve.do(lambda e: e.memset(bad, 0.0))
        count_of(0, cmp[:, :, 1:P], lambda e: e.tensor_tensor(cmp[:, :, 1:P], df[:, :, 1:P], df[:, :, 0:P - 1], ALU.is_lt))
        count_of(1, cmp, lambda e: e.tensor_scalar(cmp, rf, float(WIN), None, ALU.is_ge))
        dve.chain(lambda e: e.tensor_tensor(step[:, 0:NC - 1], FB[:, 1:NC], FB[:, 0:NC - 1], ALU.subtract))
        late = cmp.rearrange("p t e -> p (t e)")[:, 0:NC - 1]
        count_of(2, late, lambda e: e.tensor_tensor(late, REL[:, 0:NC - 1], step[:, 0:NC - 1], ALU.is_gt))
        count_of(3, late, lambda e: e.tensor_scalar(late, step[:, 0:NC - 1], 0.0, None, ALU.is_le))
        count_of(4, late, lambda e: e.tensor_scalar(late, step[:, 0:NC - 1], float(WIN), None, ALU.is_gt))
        dve.chain(lambda e: e.tensor_scalar(bad[:, 5:6], FB[:, 0:1], 0.0, None, ALU.not_equal))
        dve.chain(lambda e: e.tensor_reduce(bad[:, 7:8], bad[:, 0:7], AX_X, ALU.add))
        dve.do(lambda e: e.memset(SHARED, 0.0))
        dve.chain(lambda e: e.tensor_tensor(SHARED[:, 0:NC - 1], REL[:, 0:NC - 1], step[:, 0:NC - 1], ALU.is_equal))
        m = pe.do(lambda e: e.matmul(banks[:, 5, 0:1], ones, bad[:, 7:8], start=True, stop=True), dve.last())
        dve.do(lambda e: e.tensor_copy(FLAG, banks[:, 5, 0:1]), m)
        barrier()

        def layer_norm(X, Y, space, n=NB, ready=None):
            dve.wait(dve.last())
            stats, mv, rs = space.get([NB, 6]), space.get([NB, 2]), space.get([NB])
            for b in range(n):
                dve.do(lambda e, b=b: e.bn_stats(stats[:, b, :], X[:, b, :]), ready)
            t = dve.last()
            for b in range(n):
                dve.do(lambda e, b=b: e.bn_aggr(mv[:, b, :], stats[:, b, :]), t)
            dve.chain(lambda e: e.tensor_scalar_add(rs, mv[:, :, 1], 1e-5))
            r = act.do(lambda e: e.activation(rs, rs, ACT.Sqrt), dve.last())
            dve.chain(lambda e: e.reciprocal(rs, rs), r)
            t = dve.last()
            for b in range(n):
                dve.do(lambda e, b=b: e.tensor_scalar(Y[:, b, :], X[:, b, :], mv[:, b, 0:1], rs[:, b:b + 1],
                                                      ALU.subtract, ALU.mult), t)
            return dve.chain(lambda e: e.tensor_scalar_max(Y, Y, 0.0))

        def load_x(X):
            z = dve.do(lambda e: e.memset(X[:, NB - 1, :], 0.0))
            f = N // P
            ld.dma(sp, lambda e: e.dma_start(X[:, 0:f, :], a["x"][0:f * P, :].rearrange("(b p) f -> p b f", p=P)), z)
            return ld.dma(sp, lambda e: e.dma_start(X[0:N - f * P, f, :], a["x"][f * P:N, :]))

        def first_norm():
            s1 = Space(keep_end)
            X, Hh = s1.get([NB, D]), s1.get([NB, D])
            ready = load_x(X)
            done = layer_norm(X, Hh, s1, ready=ready)
            st.dma(sp, lambda e: e.dma_start(blocks(h_table), Hh), done)
            barrier()

        first_norm()
        gl = [landing(f"g{i}") for i in range(40)]
        env = {}

        def firsts(lane, c0, n):
            env["tags"] = tag = env.get("tags", 0) + 1

            def op(e):
                regs = [e.alloc_register(f"first{tag}_{k}") for k in range(n)]
                e.reg_load(regs, FI[0:1, c0:c0 + n])
                for k, r in enumerate(regs):
                    env[(id(lane), c0 + k)] = e.snap(r, donate=True, min_val=0, max_val=N)
                env[(id(lane), "regs")] = regs
            lane.ops.append(op)

        def release(lane):
            def op(e):
                for r in env[(id(lane), "regs")]:
                    e.free_register(r)
            lane.ops.append(op)

        def window(lane, ap, c):
            v = env[(id(lane), c)]
            if len(ap.shape) == 3:
                return ap[:, :, bass.ds(v, WIN)]
            return ap[:, bass.ds(v, WIN)]

        def layer0_edges():
            s2 = Space(keep_end)
            s2.get([NP])
            R, RX = 16, 8
            CC = NB * WIN
            CS = CC + NB
            SH = s2.get([4, NB + 1])
            G = s2.get([R, D])
            S = s2.get([R, WIN + 1])
            BY_LO = s2.get([RX, P], BF16)
            BY_HI_D = s2.get([RX, CC + 28], BF16)
            columns = s2.get([CC], I16)
            LO, HI, KEY = s2.get([NC]), s2.get([NC]), s2.get([NC])
            WS = s2.get([NC])
            LOI, HII = (v.bitcast(I32) for v in (WS, KEY))
            dve.do(lambda e: e.memset(ACC0[:, N + 1:NP], 0.0))
            dve.do(lambda e: e.memset(C[:, :, N + 1:NP], 0.0))
            pool.do(lambda e: e.iota(columns, [[1, CC]], base=0, channel_multiplier=0))
            dve.do(lambda e: e.tensor_single_scalar(LOI, SRC, P - 1, ALU.bitwise_and))
            dve.do(lambda e: e.tensor_single_scalar(HII, SRC, 7, ALU.logical_shift_right))
            dve.chain(lambda e: e.tensor_copy(LO, LOI))
            dve.do(lambda e: e.tensor_copy(HI, HII))
            dve.chain(lambda e: e.scalar_tensor_tensor(KEY, HI, float(WIN), REL, ALU.mult, ALU.add))
            dve.chain(lambda e: e.tensor_tensor(WS, WT, SHARED, ALU.mult))
            barrier()
            T = {}
            get = T.get

            def chunk(c):
                k, kx, bk = c % R, c % RX, c % 8
                g = gl[k].dma(pool, lambda e: e.indirect_dma_start(
                    G[:, k, :], None, h_table, bass.IndirectOffsetOnAxis(ap=SRC[:, c:c + 1].bitcast(U32), axis=0)), get(("free", c - R)))
                if c % 8 == 0:
                    dve.do(lambda e: e.tensor_copy(S[:, k:k + 8, 0], WS[:, c:c + 8]), get(("free", c + 7 - R)))
                dve.do(lambda e: e.tensor_scalar(BY_LO[:, kx, :], columns[:, 0:P], LO[:, c:c + 1], None, ALU.is_equal), get(("free", c - RX)))
                dve.do(lambda e: e.tensor_scalar(BY_HI_D[:, kx, CC:CC + NB], columns[:, 0:NB], HI[:, c:c + 1], SHARED[:, c:c + 1], ALU.is_equal, ALU.mult))
                x = dve.do(lambda e: e.tensor_scalar(BY_HI_D[:, kx, 0:CC], columns, KEY[:, c:c + 1], None, ALU.is_equal))
                w = dve.do(lambda e: e.tensor_scalar(S[:, k, 1:WIN + 1], iota_w, REL[:, c:c + 1], WT[:, c:c + 1], ALU.is_equal, ALU.mult))
                pe.quiet(lambda e: e.matmul(banks[:, bk, 0:CC + NB], BY_LO[:, kx, :], BY_HI_D[:, kx, 0:CC + NB], start=True, stop=True, skip_group_check=True),
                         x, get(("acc", c - 8)))
                T["free", c] = pe.do(lambda e: e.matmul(banks[:, bk, CS:CS + WIN + 1], G[:, k, :], S[:, k, :], start=False, stop=True, skip_group_check=True), g, w)

            def share(c):
                bk = c % 8
                T["kept", c] = T["shared", c] = act.do(lambda e: e.activation(SH[:, c % 4, :], banks[:, bk, CC:CS + 1], ACT.Copy),
                                                       T["free", c], get(("shared", c - 3)))
                if c:
                    dve.do(lambda e: e.tensor_tensor(banks[:, bk, 0:CC:WIN], banks[:, bk, 0:CC:WIN], SH[:, (c - 1) % 4, 0:NB], ALU.add), T["kept", c])
                    T["shared", c] = dve.do(lambda e: e.tensor_tensor(
                        banks[:, bk, CS + 1:CS + 2], banks[:, bk, CS + 1:CS + 2], SH[:, (c - 1) % 4, NB:NB + 1], ALU.add))

            def store(c):
                bk = c % 8
                T["adj", c] = act.do(lambda e: e.activation(window(act, C, c), banks[:, bk, 0:CC].rearrange("p (b w) -> p b w", w=WIN), ACT.Copy),
                                     T["shared", c], get(("adj", c - 1)))
                T["acc", c] = act.do(lambda e: e.activation(window(act, ACC0, c), banks[:, bk, CS + 1:CS + 1 + WIN], ACT.Copy), get(("acc", c - 1)))

            lag = 2
            for c in range(NC + lag):
                if c < NC:
                    chunk(c)
                if 1 <= c <= NC:
                    share(c - 1)
                if c >= lag:
                    if (c - lag) % 8 == 0:
                        if c > lag:
                            release(act)
                        firsts(act, c - lag, 8)
                    store(c - lag)
            release(act)
            barrier()
            adj_saved = landing("adj_saved")
            adj_saved.dma(act, lambda e: e.dma_start(adj_rows, CF))

        def groups(width=4):
            return [(b, min(width, NB - b)) for b in range(0, NB, width)]

        def load_row(z, v, row):
            return z.dma(sp, lambda e: e.dma_start(v, row.partition_broadcast(P)))

        def row_of(ap):
            while len(ap.shape) > 1:
                ap = ap[0]
            return ap

        def layer0_nodes():
            s3 = Space(keep_end)
            s3.get([NP])
            X, Hh = s3.get([NB, D]), s3.get([NB, D])
            W0, B0 = s3.get([D]), s3.get([D])
            ld2.dma(sp, lambda e: e.dma_start(W0, a["L0_gnn_weight"]))
            wready = load_row(ld2, B0, a["L0_gnn_bias"])
            xready = load_x(X)
            freed = {}
            for g, (b0, n) in enumerate(groups()):
                bk = g % 4
                for b in range(b0, b0 + n):
                    m = pe.do(lambda e, b=b, b0=b0, bk=bk: e.matmul(
                        banks[:, bk, (b - b0) * D:(b - b0 + 1) * D], ACC0[:, b * P:(b + 1) * P], W0, start=True, stop=True),
                        wready, freed.get(g - 4))
                xs = X[:, b0:b0 + n, :]
                u = dve.do(lambda e, xs=xs, bk=bk, n=n: e.tensor_tensor(
                    xs, xs, banks[:, bk, 0:n * D].rearrange("p (b f) -> p b f", f=D), ALU.add), m, xready)
                freed[g] = u
            dve.chain(lambda e: e.tensor_tensor(X, X, B0.unsqueeze(1).broadcast_to([P, NB, D]), ALU.add))
            done = layer_norm(X, Hh, s3)
            st.dma(sp, lambda e: e.dma_start(blocks(x_rows), X), done)
            st.dma(sp, lambda e: e.dma_start(blocks(h_rows), Hh))
            barrier()


        def split3(src, parts, tmp, *waits):
            hi, mid, lo = parts
            dve.do(lambda e: e.tensor_copy(hi, src), *waits)
            dve.chain(lambda e: e.tensor_tensor(tmp, src, hi, ALU.subtract))
            dve.chain(lambda e: e.tensor_copy(mid, tmp))
            return dve.chain(lambda e: e.tensor_tensor(lo, tmp, mid, ALU.subtract))

        def layer1_sums():
            s4 = Space(keep_end)
            s4.get([NP])
            U = s4.get([NB, 3 * D], BF16)
            s4.get([NB])
            Hl = s4.get([5, D])
            ct_at = s4.word
            tmp = s4.get([5, D])
            NH = [13, 12]
            for q in range(0, NB, 5):
                hr = ld.dma(sp, lambda e, q=q: e.dma_start(Hl, blocks(h_rows)[:, q:q + 5, :]), dve.last())
                split3(Hl, [U[:, q:q + 5, k * D:(k + 1) * D] for k in range(3)], tmp, hr)
            udone = dve.last()
            s4 = Space(ct_at)
            CT = [s4.get([NH[0] * P], BF16) for _ in range(2)]
            it = 0
            ct_free, bank_free = {}, {}
            agg_free = None
            for half in range(2):
                nh = NH[half]
                sb0 = half * NH[0]
                w = nh * P
                for db in range(NB):
                    k = it % 2
                    tb = 4 + 2 * k
                    for i in range(nh):
                        bank, col = tb + i // 8, (i % 8) * P
                        m = pe.do(lambda e, i=i, bank=bank, col=col, db=db, sb0=sb0: e.transpose(
                            banks[:, bank, :].bitcast(BF16)[:, col:col + P], C[:, sb0 + i, db * P:(db + 1) * P], identb),
                            bank_free.get(it - 2))
                    e1 = act.do(lambda e, k=k, tb=tb: e.activation(CT[k][:, 0:8 * P], banks[:, tb, :].bitcast(BF16), ACT.Copy),
                                m, ct_free.get(it - 2), udone)
                    e2 = dve.do(lambda e, k=k, tb=tb, w=w: e.tensor_copy(CT[k][:, 8 * P:w], banks[:, tb + 1, :].bitcast(BF16)[:, 0:w - 8 * P]),
                                m, ct_free.get(it - 2), udone)
                    if it % 2 == 0:
                        dve.do(lambda e, b=it // 2: e.tensor_reduce(odeg[:, b:b + 1], C[:, b, :], AX_X, ALU.add))
                    pend = (e1, e2)
                    def products(it, half, db, w, pend):
                        k = it % 2
                        for j in range(3):
                            for c in range(0, w, 512):
                                n = min(512, w - c)
                                m = pe.do(lambda e, j=j, c=c, n=n, db=db, k=k: e.matmul(
                                    banks[:, c // 512, 0:n], U[:, db, j * D:(j + 1) * D], CT[k][:, c:c + n],
                                    start=(db == 0 and j == 0), stop=(db == NB - 1 and j == 2), skip_group_check=True), *pend, udone, agg_free)
                        ct_free[it] = m
                        return m
                    bank_free[it] = None
                    if db:
                        products(it - 1, half, db - 1, w, prevp)
                    prevp = pend
                    bank_free[it] = e1
                    bank_free[it + 0.5] = e2
                    it += 1
                    pe.wait(bank_free.get(it - 2), bank_free.get(it - 1.5))
                m = products(it - 1, half, NB - 1, w, prevp)
                for c in range(0, w, 512):
                    n = min(512, w - c)
                    agg_free = act.do(lambda e, c=c, n=n, sb0=sb0: e.activation(AGG[:, sb0 * P + c:sb0 * P + c + n], banks[:, c // 512, 0:n], ACT.Copy), m)
            barrier()


        def layer1_nodes():
            s5 = Space(keep_end + NP)
            X = s5.get([NB, D])
            s5 = Space(keep_end + 2 * NP, keep_end + NP + NB * 3 * D // 2)
            Wl, Wr, Bl, Br = (s5.get([D]) for _ in range(4))
            rd, nrm = s5.get([NB]), s5.get([NB])
            t2 = [s5.get([4, D])]
            s5 = Space(keep_end + NP + NB * 3 * D // 2 + NB)
            Hl = [s5.get([4, D]) for _ in range(2)]
            Ht = [s5.get([4 * D]) for _ in range(2)]
            ld2.dma(sp, lambda e: e.dma_start(Wl, a["L1_gnn_Wl"]))
            ld2.dma(sp, lambda e: e.dma_start(Wr, a["L1_gnn_Wr"]))
            load_row(ld2, Bl, a["L1_gnn_bl"])
            wready = load_row(ld2, Br, a["L1_gnn_br"])
            xready = ld.dma(sp, lambda e: e.dma_start(X, blocks(x_rows)))
            dve.do(lambda e: e.tensor_tensor(Bl, Bl, Br, ALU.add), wready)
            dve.do(lambda e: e.tensor_scalar_max(rd, odeg, 1.0))
            dve.chain(lambda e: e.reciprocal(rd, rd))
            hl = [landing("hl0"), landing("hl1")]
            ht_free, hl_free, bank_free, t2_free = {}, {}, {}, None
            for g, (b0, n) in enumerate(groups()):
                k = g % 2
                hr = hl[k].dma(sp, lambda e, b0=b0, n=n, k=k: e.dma_start(Hl[k][:, 0:n, :], blocks(h_rows)[:, b0:b0 + n, :]), hl_free.get(g - 2))
                for i in range(n):
                    m = pe.do(lambda e, i=i, k=k: e.transpose(banks[:, 6 + k, i * P:(i + 1) * P], Hl[k][:, i, :], ident), hr, ht_free.get(g - 2))
                hl_free[g] = m
                hc = act.do(lambda e, k=k, n=n: e.activation(Ht[k][:, 0:n * P], banks[:, 6 + k, 0:n * P], ACT.Copy), m, ht_free.get(g - 2))
                for i in range(n):
                    b = b0 + i
                    pe.do(lambda e, i=i, k=k: e.matmul(banks[:, k, i * D:(i + 1) * D], Ht[k][:, i * P:(i + 1) * P], Wl, start=True, stop=True), hc, wready, bank_free.get(g - 2))
                    m = pe.do(lambda e, i=i, k=k, b=b: e.matmul(banks[:, 2 + k, i * D:(i + 1) * D], AGG[:, b * P:(b + 1) * P], Wr, start=True, stop=True))
                ht_free[g] = m
                v = t2[0][:, 0:n, :]
                p1 = banks[:, k, 0:n * D].rearrange("p (b f) -> p b f", f=D)
                p2 = banks[:, 2 + k, 0:n * D].rearrange("p (b f) -> p b f", f=D)
                dve.do(lambda e, v=v, p2=p2, b0=b0, n=n: e.tensor_tensor(v, p2, rd[:, b0:b0 + n].unsqueeze(2).broadcast_to([P, n, D]), ALU.mult), dve.last(), m, t2_free)
                dve.chain(lambda e, v=v, p1=p1: e.tensor_tensor(v, v, p1, ALU.add))
                bank_free[g] = dve.last()
                dve.chain(lambda e, v=v, n=n: e.tensor_tensor(v, v, Bl.unsqueeze(1).broadcast_to([P, n, D]), ALU.add))
                r = dve.chain(lambda e, v=v: e.tensor_scalar_max(v, v, 0.0))
                for i in range(n):
                    sq = act.do(lambda e, i=i, b=b0 + i, k=k, v=v: e.activation(Hl[k][:, i, :], v[:, i, :], ACT.Square, accum_out=nrm[:, b:b + 1]), r)
                hl_free[g] = sq
                q = act.do(lambda e, b0=b0, n=n: e.activation(nrm[:, b0:b0 + n], nrm[:, b0:b0 + n], ACT.Sqrt), sq)
                dve.do(lambda e, b0=b0, n=n: e.tensor_scalar_add(nrm[:, b0:b0 + n], nrm[:, b0:b0 + n], 1e-6), q)
                dve.chain(lambda e, b0=b0, n=n: e.reciprocal(nrm[:, b0:b0 + n], nrm[:, b0:b0 + n]))
                dve.chain(lambda e, v=v, b0=b0, n=n: e.tensor_tensor(v, v, nrm[:, b0:b0 + n].unsqueeze(2).broadcast_to([P, n, D]), ALU.mult))
                xs = X[:, b0:b0 + n, :]
                dve.chain(lambda e, v=v, xs=xs: e.tensor_tensor(xs, xs, v, ALU.add), xready)
                t2_free = dve.last()
            barrier()
            s6 = Space(keep_end)
            H2 = s6.get([NB, D])
            s6 = Space(keep_end + 2 * NP)
            layer_norm(X, H2, s6)
            st.dma(sp, lambda e: e.dma_start(blocks(x_rows), X), dve.last())
            barrier()


        RING = 40
        ACC = at(0, [H + 1, NP])
        SACC = at(keep_end, [NP], parts=H + 1)
        ring_at = (H + 1) * NP
        X1, X2 = at(ring_at, [NB, D]), at(ring_at + NP, [NB, D])
        node_at = keep_end + NP
        gat = [{k: a[f"L2_gnn_{v}"] for k, v in (("W", f"gat_W{i}"), ("src", f"gat_a{i}_src"), ("dst", f"gat_a{i}_dst"))}
               for i in range(2)]

        def scores(i, Hn, V, ES, space):
            K = D // H if i == 0 else D
            Wg, av, pr = (space.get([H, K]) for _ in range(3))
            Ht = [space.get([4 * D]) for _ in range(2)]
            w = ld2.dma(sp, lambda e: e.dma_start(Wg, gat[i]["W"].rearrange("h f k -> f h k")), dve.last(), pe.last())
            for j, k in enumerate(("src", "dst")):
                r = ld2.dma(sp, lambda e, k=k: e.dma_start(av.rearrange("p h k -> p (h k)"), gat[i][k].rearrange("h k -> (h k)").partition_broadcast(P)), dve.last())
                dve.do(lambda e: e.tensor_tensor(pr, Wg, av, ALU.mult), r, dve.last())
                dve.chain(lambda e, j=j: e.tensor_reduce(V[:, j * H:(j + 1) * H], pr, AX_X, ALU.add))
            vt = dve.last()
            hfree, bfree = {}, {}
            for g, (b0, n) in enumerate(groups()):
                k = g % 2
                for q in range(n):
                    m = pe.do(lambda e, q=q, k=k, b0=b0: e.transpose(banks[:, 6 + k, q * P:(q + 1) * P], Hn[:, b0 + q, :], ident), vt, hfree.get(g - 2))
                hc = act.do(lambda e, k=k, n=n: e.activation(Ht[k][:, 0:n * P], banks[:, 6 + k, 0:n * P], ACT.Copy), m, bfree.get(g - 2), vt)
                hfree[g] = hc
                for q in range(n):
                    m = pe.do(lambda e, q=q, k=k: e.matmul(banks[:, 4 + k, q * 2 * H:(q + 1) * 2 * H], Ht[k][:, q * P:(q + 1) * P], V, start=True, stop=True), hc, bfree.get(g - 2))
                bfree[g] = dve.do(lambda e, k=k, n=n, b0=b0: e.tensor_copy(ES[:, b0:b0 + n, :], banks[:, 4 + k, 0:n * 2 * H].rearrange("p (b s) -> p b s", s=2 * H)), m)
            return dve.last()

        def layer2_tables0():
            H2 = at(keep_end, [NB, D])
            space = Space(keep_end + NP)
            V, ES = space.get([2 * H]), space.get([NB, 2 * H])
            done = scores(0, H2, V, ES, space)
            st.dma(sp, lambda e: e.dma_start(blocks(gat0_table)[:, :, 0:D], H2), done)
            st.dma(sp, lambda e: e.dma_start(blocks(gat0_table)[:, :, D:D + H], ES[:, :, 0:H]))
            st.dma(sp, lambda e: e.dma_start(blocks(ed_table[0]), ES[:, :, H:2 * H]))
            barrier()

        def layer2_edges(i):
            table, row = (gat0_table, D + H) if i == 0 else (gat1_table, 2 * D + H)
            space = Space(node_at)
            G = at(ring_at, [RING, row])
            R4, R3, RS = 4, 3, 4
            OH = [space.get([WIN + 1, BC]) for _ in range(R4)]
            OT = [space.get([P]) for _ in range(2)]
            EDR = [space.get([H]) for _ in range(R4)]
            BD = [space.get([BC, H]) for _ in range(2)]
            DLI = [space.get([P + 2], I32, 64) for _ in range(2)]
            DLF = [space.get([P + 2], parts=64) for _ in range(2)]
            EQ = [space.get([P + 1], parts=64) for _ in range(2)]
            MF, MN = ([space.get([P], parts=64) for _ in range(R3)] for _ in range(2))
            Z = [space.get([64]) for _ in range(2)]
            ZT = [space.get([P], parts=64) for _ in range(R3)]
            FW = space.get([P], parts=64)
            ML = [space.get([P], parts=64) for _ in range(R4)]
            MM = space.get([P], parts=64)
            DF = [space.get([P], parts=64) for _ in range(2)]
            A = [space.get([BC, H + 1]) for _ in range(R3)]
            S = [space.get([H + 1, WIN + 1]) for _ in range(RS)]
            SH = [space.get([H + 1]) for _ in range(4)]
            SHW = [space.get([1], parts=H + 1) for _ in range(4)]
            PS = 160
            dve.do(lambda e: e.memset(ACC[:, :, N + 1:NP], 0.0))
            dve.do(lambda e: e.memset(SACC[:, N + 1:NP], 0.0))
            zero = dve.last()
            dl = [landing(f"dl{i}_{k}") for k in range(2)]
            edl = [landing(f"ed{i}_{k}") for k in range(2 * R4)]
            T = {}
            get = T.get

            def gathers(b):
                T["ed", b] = edl[b % (2 * R4)].dma(pool, lambda e: e.indirect_dma_start(
                    EDR[b % R4], None, ed_table[i], bass.IndirectOffsetOnAxis(ap=EDI[:, b:b + 1].bitcast(U32), axis=0)),
                    get(("bd", b - R4)))
                for c in range(BC * b, BC * b + BC):
                    T["g", c] = gl[c % RING].dma(pool, lambda e, c=c: e.indirect_dma_start(
                        G[:, c % RING, :], None, table, bass.IndirectOffsetOnAxis(ap=SRC[:, c:c + 1].bitcast(U32), axis=0)),
                        get(("mm", c - RING)))

            def rows_of(b):
                src = dst_flat[0, b * BC * P:b * BC * P + 1]
                ap = bass.AP(tensor=dst_flat.tensor, offset=b * BC * P, ap=[[P, BC], [0, H], [1, P + 2]])
                T["dl", b] = dl[b % 2].dma(sp, lambda e, b=b, ap=ap: e.dma_start(DLI[b % 2], ap), get(("dlf", b - 2)))

            def s1(b):
                k4, k3, k2 = b % R4, b % R3, b % 2
                c0 = b * BC

                def one_hot():
                    dve.do(lambda e: e.tensor_copy(OH[k4][:, WIN, :], SHARED[:, c0:c0 + BC]),
                           get(("mm", c0 + BC - 1 - R4 * BC)), get(("sm", c0 + BC - 1 - R4 * BC)), get(("tr", b - R4)))
                    T["oh", b] = dve.do(lambda e: e.tensor_tensor(
                        OH[k4][:, 0:WIN, :], iota_w.unsqueeze(2).broadcast_to([P, WIN, BC]),
                        REL[:, c0:c0 + BC].unsqueeze(1).broadcast_to([P, WIN, BC]), ALU.is_equal))
                    T["dlf", b] = dve.do(lambda e: e.tensor_copy(DLF[k2], DLI[k2]), T["dl", b], get(("flags", b - 2)))

                def turn():
                    T["tr", b] = pe.do(lambda e: e.transpose(banks[:, 0, 0:P], OH[k4][:, 0:WIN, :].rearrange("p w c -> p (w c)"), ident),
                                       T["oh", b], get(("ot", b - 1)))
                    T["ot", b] = act.do(lambda e: e.activation(OT[k2], banks[:, 0, 0:P], ACT.Copy), T["tr", b], get(("edm", b - 2)))

                def flags():
                    d = DLF[k2]
                    dve.do(lambda e: e.tensor_tensor(EQ[k2], d[:, 0:P + 1], d[:, 1:P + 2], ALU.not_equal), T["dlf", b], get(("bw", b - 2)))
                    dve.do(lambda e: e.tensor_scalar(MF[k3], d[:, 1:P + 1], d[:, 0:1], -BIG, ALU.not_equal, ALU.mult), get(("m", b - R3)))
                    dve.do(lambda e: e.tensor_scalar(MN[k3], d[:, 1:P + 1], d[:, P + 1:P + 2], -BIG, ALU.not_equal, ALU.mult))
                    T["flags", b] = dve.chain(lambda e: e.tensor_scalar(EQ[k2], EQ[k2], -BIG, None, ALU.mult))

                def expand():
                    T["bd", b] = dve.do(lambda e: e.tensor_tensor(
                        BD[k2], EDR[k4].unsqueeze(1).broadcast_to([P, BC, H]), slot_mask.unsqueeze(2).broadcast_to([P, BC, H]), ALU.mult),
                        T["ed", b], get(("edm", b - 2)))
                    T["edm", b] = pe.do(lambda e: e.matmul(banks[:, 1, 0:BC * H], OT[k2], BD[k2].rearrange("p j h -> p (j h)"), start=True, stop=True),
                                        T["ot", b], T["bd", b], get(("z", b - 1)))

                def logits():
                    s = c0 % RING
                    z = Z[k2].rearrange("p (c h) -> p c h", h=H)
                    T["z", b] = dve.do(lambda e: e.tensor_tensor(
                        z, banks[:, 1, 0:BC * H].rearrange("p (c h) -> p c h", h=H), G[:, s:s + BC, D:D + H], ALU.add),
                        T["edm", b], *[T["g", c] for c in range(c0, c0 + BC)], get(("zt", b - 2)))
                    T["zr", b] = dve.chain(lambda e: e.scalar_tensor_tensor(Z[k2], Z[k2], 0.2, Z[k2], ALU.mult, ALU.max))

                def turn_logits():
                    T["zt", b] = pe.do(lambda e: e.transpose(banks[0:64, 2, 0:P], Z[k2], ident), T["zr", b], get(("ztc", b - 1)))
                    T["ztc", b] = act.do(lambda e: e.activation(ZT[k3], banks[0:64, 2, 0:P], ACT.Copy), T["zt", b], get(("d", b - R3)), get(("bw", b - R3)))

                def scans():
                    dve.do(lambda e: e.tensor_tensor_scan(FW, EQ[k2][:, 0:P], ZT[k3], -BIG, ALU.add, ALU.max), T["ztc", b], T["flags", b], dve.last())
                    T["bw", b] = dve.do(lambda e: e.tensor_tensor_scan(ML[k4][:, ::-1], EQ[k2][:, P:0:-1], FW[:, ::-1], -BIG, ALU.add, ALU.max),
                                        dve.last(), get(("ex", b - R4 + 1)), get(("m", b - R4)))

                return [one_hot, turn, flags, expand, logits, turn_logits, scans]

            def s2(b):
                k4, k3, k2 = b % R4, b % R3, b % 2

                def exchange():
                    me = ML[k4]
                    pr = ML[(b - 1) % R4] if b else None
                    ne = ML[(b + 1) % R4] if b < NBATCH - 1 else None
                    w = (T["bw", b], get(("bw", b + 1)), get(("m", b - 1)))
                    o = banks[0:64, 3, 0:2]
                    pe.do(lambda e: e.matmul(o[:, 0:1], wide[0:64, P - H:P - H + 64], me[:, P - 1:P], start=True, stop=pr is None), *w)
                    if pr is not None:
                        pe.do(lambda e: e.matmul(o[:, 0:1], wide[0:64, P + 64 - H:P + 128 - H], pr[:, P - 1:P], start=False, stop=True))
                    T["ex", b] = pe.do(lambda e: e.matmul(o[:, 1:2], wide[0:64, P + H:P + H + 64], me[:, 0:1], start=True, stop=ne is None))
                    if ne is not None:
                        T["ex", b] = pe.do(lambda e: e.matmul(o[:, 1:2], wide[0:64, P - 64 + H:P + H], ne[:, 0:1], start=False, stop=True))

                def maxima():
                    o = banks[0:64, 3, 0:2]
                    c0 = b * BC
                    T["aw", b] = dve.do(lambda e: e.tensor_copy(A[k3][:, :, H], WT[:, c0:c0 + BC]), get(("sg", c0 + BC - 1 - R3 * BC)), get(("sm", c0 + BC - 1 - R3 * BC)))
                    dve.do(lambda e: e.scalar_tensor_tensor(MM, MF[k3], o[:, 0:1], ML[k4], ALU.add, ALU.max), T["ex", b], dve.last())
                    T["m", b] = dve.chain(lambda e: e.scalar_tensor_tensor(MM, MN[k3], o[:, 1:2], MM, ALU.add, ALU.max))
                    T["d", b] = dve.chain(lambda e: e.tensor_tensor(DF[k2], ZT[k3], MM, ALU.subtract), get(("p", b - 2)))

                def expo():
                    x = act.do(lambda e: e.activation(DF[k2], DF[k2], ACT.Exp), T["d", b])
                    T["p", b] = pe.do(lambda e: e.transpose(banks[:, 3, P:P + 64], DF[k2], ident[0:64, 0:64]), x, get(("a", b - 1)))
                    T["a", b] = act.do(lambda e: e.activation(A[k3][:, :, 0:H], banks[:, 3, P:P + 64].rearrange("p (c h) -> p c h", h=H), ACT.Copy),
                                       T["p", b], get(("sg", b * BC + BC - 1 - R3 * BC)), get(("sm", b * BC + BC - 1 - R3 * BC)))

                return [exchange, maxima, expo]

            def share(c):
                bk = 4 + c % 4
                pv = banks[:, bk, 0:(H + 1) * (WIN + 1)].rearrange("p (h w) -> p h w", w=WIN + 1)
                act.do(lambda e: e.activation(SH[c % 4], pv[:, :, WIN], ACT.Copy), T["sm", c], get(("shared", c - 3)))
                T["kept", c] = T["shared", c] = act.do(lambda e: e.activation(SHW[c % 4], banks[0:H + 1, bk, PS + WIN:PS + WIN + 1], ACT.Copy))
                if c:
                    dve.do(lambda e: e.tensor_tensor(pv[:, :, 0], pv[:, :, 0], SH[(c - 1) % 4], ALU.add), T["kept", c])
                    T["shared", c] = dve.do(lambda e: e.tensor_tensor(
                        banks[0:H + 1, bk, PS:PS + 1], banks[0:H + 1, bk, PS:PS + 1], SHW[(c - 1) % 4], ALU.add))

            def store(c):
                bk = 4 + c % 4
                pv = banks[:, bk, 0:(H + 1) * (WIN + 1)].rearrange("p (h w) -> p h w", w=WIN + 1)
                T["acc", c] = act.do(lambda e: e.activation(window(act, ACC, c), pv[:, :, 0:WIN], ACT.Copy),
                                     T["shared", c], get(("acc", c - 1)), zero)
                T["sacc", c] = act.do(lambda e: e.activation(window(act, SACC, c), banks[0:H + 1, bk, PS:PS + WIN], ACT.Copy), get(("sacc", c - 1)))

            def chunk(b, j):
                c = b * BC + j
                k4, k3, ks = b % R4, b % R3, c % RS
                pv = banks[:, 4 + c % 4, 0:(H + 1) * (WIN + 1)]
                cut = H * (WIN + 1)

                def op():
                    T["sg", c] = dve.do(lambda e: e.tensor_tensor(
                        S[ks], OH[k4][:, :, j].unsqueeze(1).broadcast_to([P, H + 1, WIN + 1]),
                        A[k3][:, j, :].unsqueeze(2).broadcast_to([P, H + 1, WIN + 1]), ALU.mult),
                        T["a", b], T["aw", b], T["oh", b], get(("mm", c - RS)))
                    sv = S[ks].rearrange("p h w -> p (h w)")
                    g = G[:, c % RING, :]
                    waits = (T["sg", c], T["g", c], get(("sacc", c - 4)))
                    if i == 0:
                        T["mm", c] = pe.do(lambda e: e.matmul(pv, g[:, 0:D], sv, start=True, stop=True, skip_group_check=True), *waits)
                    else:
                        pe.quiet(lambda e: e.matmul(pv[:, 0:cut], g[:, 0:D], sv[:, 0:cut], start=True, stop=True, skip_group_check=True), *waits)
                        T["mm", c] = pe.do(lambda e: e.matmul(pv[:, cut:], g[:, D + H:], sv[:, cut:], start=False, stop=True, skip_group_check=True))
                    T["sm", c] = pe.do(lambda e: e.matmul(banks[0:H + 1, 4 + c % 4, PS:PS + WIN + 1], A[k3][:, j, :], OH[k4][:, :, j],
                                                          start=False, stop=True, skip_group_check=True))
                    if c:
                        share(c - 1)
                    if c > 1:
                        store(c - 2)
                    if j == 1:
                        if b:
                            release(act)
                        firsts(act, c - 1, BC)
                return op

            SLOTS, AFTER = 10, 2
            sums_at = {SLOTS * (b + 2) + AFTER + j * SLOTS // BC: chunk(b, j) for b in range(NBATCH) for j in range(BC)}
            for p in range(NBATCH + 3):
                if p < NBATCH:
                    rows_of(p)
                    gathers(p)
                steps = (s1(p) if p < NBATCH else [None] * 7) + (s2(p - 1) if 1 <= p <= NBATCH else [None] * 3)
                for q, step in enumerate(steps):
                    if SLOTS * p + q in sums_at:
                        sums_at[SLOTS * p + q]()
                    if step is not None:
                        step()
            share(NC - 1)
            store(NC - 2)
            store(NC - 1)
            release(act)
            barrier()

        def weight_sums(space, SV):
            for b in range(NB):
                m = pe.do(lambda e, b=b: e.transpose(banks[:, 0, b * (H + 1):(b + 1) * (H + 1)], SACC[:, b * P:(b + 1) * P], ident[0:H + 1, 0:H + 1]))
            dve.do(lambda e: e.tensor_scalar_max(SV, banks[:, 0, 0:NB * (H + 1)].rearrange("p (b h) -> p b h", h=H + 1), 1e-16), m)
            return dve.chain(lambda e: e.reciprocal(SV, SV))

        def layer2_nodes0():
            K = D // H
            space = Space(node_at)
            SV = space.get([NB, H + 1])
            Wg, Wc = space.get([H, K]), space.get([D])
            ld2.dma(sp, lambda e: e.dma_start(Wg, gat[0]["W"].rearrange("h f k -> f h k")))
            w = ld2.dma(sp, lambda e: e.dma_start(Wc, a["L2_gnn_gcn_W0"]))
            weight_sums(space, SV)
            bfree = {}
            for g, (b0, n) in enumerate(groups()):
                k = g % 2
                for q in range(n):
                    b = b0 + q
                    for h in range(H):
                        pe.quiet(lambda e, b=b, q=q, h=h, k=k: e.matmul(
                            banks[:, 2 + k, q * D + h * K:q * D + (h + 1) * K], ACC[:, h, b * P:(b + 1) * P], Wg[:, h, :], start=True, stop=True), w, bfree.get(g - 2))
                    m = pe.do(lambda e, b=b, q=q, k=k: e.matmul(banks[:, 4 + k, q * D:(q + 1) * D], ACC[:, H, b * P:(b + 1) * P], Wc, start=True, stop=True))
                dve.do(lambda e, b0=b0, n=n, k=k: e.tensor_tensor(
                    X1[:, b0:b0 + n, :].rearrange("p b (h k) -> p b h k", h=H), banks[:, 2 + k, 0:n * D].rearrange("p (b h k) -> p b h k", h=H, k=K),
                    SV[:, b0:b0 + n, 0:H].unsqueeze(3).broadcast_to([P, n, H, K]), ALU.mult), m, dve.last())
                bfree[g] = dve.do(lambda e, b0=b0, n=n, k=k: e.tensor_tensor(
                    X2[:, b0:b0 + n, :], banks[:, 4 + k, 0:n * D].rearrange("p (b f) -> p b f", f=D),
                    SV[:, b0:b0 + n, H:H + 1].broadcast_to([P, n, D]), ALU.mult))
            EX = space.get([NB, D])
            dve.chain(lambda e: e.tensor_scalar_max(X2, X2, 0.0))
            t = dve.do(lambda e: e.tensor_scalar_min(EX, X1, 0.0))
            t = act.do(lambda e: e.activation(EX, EX, ACT.Exp), t)
            dve.do(lambda e: e.tensor_scalar_add(EX, EX, -1.0), t)
            dve.chain(lambda e: e.scalar_tensor_tensor(X1, X1, 0.0, EX, ALU.max, ALU.add))
            barrier()
            V = at(node_at, [2 * H])
            ES = at(node_at + 2 * H, [NB, 2 * H])
            done = scores(1, X1, V, ES, Space(node_at + 2 * H * (NB + 1)))
            st.dma(sp, lambda e: e.dma_start(blocks(gat1_table)[:, :, 0:D], X1), done)
            st.dma(sp, lambda e: e.dma_start(blocks(gat1_table)[:, :, D:D + H], ES[:, :, 0:H]))
            st.dma(sp, lambda e: e.dma_start(blocks(gat1_table)[:, :, D + H:], X2))
            st.dma(sp, lambda e: e.dma_start(blocks(ed_table[1]), ES[:, :, H:2 * H]))
            barrier()

        def layer2_nodes1():
            space = Space(node_at)
            SV = space.get([NB, H + 1])
            Wg, Wc = space.get([H, D]), space.get([D])
            PR = [space.get([H, D]) for _ in range(2)]
            C2 = space.get([NB, D])
            ld2.dma(sp, lambda e: e.dma_start(Wg, gat[1]["W"].rearrange("h f k -> f h k")))
            w = ld2.dma(sp, lambda e: e.dma_start(Wc, a["L2_gnn_gcn_W1"]))
            xr = ld.dma(sp, lambda e: e.dma_start(X1, blocks(x_rows)))
            weight_sums(space, SV)
            dve.chain(lambda e: e.tensor_scalar_mul(SV[:, :, 0:H], SV[:, :, 0:H], 1.0 / H))
            bfree = {}
            for b in range(NB):
                k = b % 2
                for h in range(H):
                    pe.quiet(lambda e, b=b, h=h, k=k: e.matmul(
                        banks[:, 2 + 2 * k + h // 4, (h % 4) * D:(h % 4 + 1) * D], ACC[:, h, b * P:(b + 1) * P], Wg[:, h, :], start=True, stop=True), w, bfree.get(b - 2))
                m = pe.do(lambda e, b=b, k=k: e.matmul(banks[:, 6 + k, 0:D], ACC[:, H, b * P:(b + 1) * P], Wc, start=True, stop=True))
                dve.do(lambda e, b=b, k=k: e.tensor_tensor(
                    PR[k], banks[:, 2 + 2 * k:4 + 2 * k, :].rearrange("p a (h f) -> p (a h) f", f=D),
                    SV[:, b, 0:H].unsqueeze(2).broadcast_to([P, H, D]), ALU.mult), m, dve.last())
                bfree[b] = dve.do(lambda e, b=b, k=k: e.tensor_scalar(C2[:, b, :], banks[:, 6 + k, 0:D], SV[:, b, H:H + 1], 0.0, ALU.mult, ALU.max))
                dve.do(lambda e, b=b, k=k: e.tensor_reduce(X2[:, b, :], PR[k].rearrange("p h f -> p f h"), AX_X, ALU.add), dve.last())
            dve.chain(lambda e: e.tensor_tensor(X2, X2, C2, ALU.max))
            dve.chain(lambda e: e.tensor_tensor(X1, X1, X2, ALU.add), xr)
            layer_norm(X1, X2, Space(node_at + NB * (H + 1)))
            st.dma(sp, lambda e: e.dma_start(blocks(x_rows), X1), dve.last())
            st.dma(sp, lambda e: e.dma_start(blocks(h_rows), X2))
            barrier()


        def layer3(diffusion):
            restored = landing("adj_restored")
            c_ready = restored.dma(act, lambda e: e.dma_start(CF, adj_rows)) if diffusion is None else None
            space = Space(tables_at)
            UU = [space.get([NB, 3 * D], BF16) for _ in range(2)]
            TB = space.get([STEPS, D])
            dinv, dinv2 = space.get([NB]), space.get([NB])
            R = 3
            HB = [space.get([D]) for _ in range(R)]
            TX = [space.get([D]) for _ in range(R)]
            UF = [space.get([D]) for _ in range(2)]
            R1 = [space.get([D]) for _ in range(2)]
            tn, tm = space.get([STEPS]), space.get([2])
            tr = ld2.dma(sp, lambda e: e.dma_start(tn, a["L3_gnn_t"].rearrange("k f -> f k")))
            dve.do(lambda e: e.tensor_reduce(tm[:, 0:1], tn, AX_X, ALU.max), tr)
            x = dve.chain(lambda e: e.tensor_scalar(tn, tn, tm[:, 0:1], None, ALU.subtract))
            x = act.do(lambda e: e.activation(tn, tn, ACT.Exp), x)
            dve.do(lambda e: e.tensor_reduce(tm[:, 1:2], tn, AX_X, ALU.add), x)
            dve.chain(lambda e: e.reciprocal(tm[:, 1:2], tm[:, 1:2]))
            x = dve.chain(lambda e: e.tensor_scalar(tn, tn, tm[:, 1:2], None, ALU.mult))
            for k in range(STEPS):
                m = pe.do(lambda e, k=k: e.matmul(banks[:, 1 + k // 4, (k % 4) * D:(k % 4 + 1) * D], tn[:, k:k + 1].broadcast_to([P, P]), ident, start=True, stop=True), x)
            dve.do(lambda e: e.tensor_copy(TB.rearrange("p k f -> p (k f)"), banks[:, 1:4, :].rearrange("p a f -> p (a f)")[:, 0:STEPS * D]), m)
            Y = at(tables_at, [NB, D])
            T = {}
            get = T.get

            def windows():
                for db in range(NB):
                    for sb in range(NB):
                        m = pe.do(lambda e, db=db, sb=sb: e.matmul(banks[:, 0, db:db + 1], C[:, sb, db * P:(db + 1) * P], onesb[:, 0:1],
                                                                   start=(sb == 0), stop=(sb == NB - 1), skip_group_check=True), c_ready)
                dve.chain(lambda e: e.tensor_scalar_add(dinv2, banks[:, 0, 0:NB], 1.0), m)
                x = act.do(lambda e: e.activation(dinv, dinv2, ACT.Sqrt), dve.last())
                dve.do(lambda e: e.reciprocal(dinv, dinv), x)
                dve.do(lambda e: e.reciprocal(dinv2, dinv2), dve.last())
                scales = dve.last()

                hb = [landing(f"hb{k}") for k in range(R)]
                n = 0
                for k in range(STEPS - 1, -1, -1):
                    new, old = UU[k % 2], UU[(k + 1) % 2]
                    for db in range(NB):
                        r, r2, bk = n % R, n % 2, n % 6
                        T["hb", n] = hb[r].dma(sp, lambda e, r=r, db=db: e.dma_start(HB[r], h_rows[db * P:(db + 1) * P, :]), get(("t", n - R)))
                        T["t", n] = pool.do(lambda e, r=r, k=k: e.tensor_tensor(TX[r], HB[r], TB[:, k, :], ALU.mult), T["hb", n], scales, get(("u", n - R)))
                        if k:
                            T["tx", n] = pool.do(lambda e, r=r, db=db: e.tensor_scalar(TX[r], TX[r], dinv[:, db:db + 1], None, ALU.mult), T["t", n])
                        else:
                            T["tx", n] = T["t", n]
                        if k < STEPS - 1:
                            acc = banks[:, bk, 0:3 * D]
                            pe.quiet(lambda e, acc=acc, old=old, db=db: e.matmul(acc, identb, old[:, db, :], start=True, stop=False),
                                     T["split", n - NB - db + NB - 1], get(("red", n - 6)), scales)
                            for sb in range(NB):
                                f = lambda e, acc=acc, old=old, db=db, sb=sb: e.matmul(acc, C[:, sb, db * P:(db + 1) * P], old[:, sb, :], start=False, stop=(sb == NB - 1))
                                if sb < NB - 1:
                                    pe.quiet(f)
                            T["mm", n] = pe.do(f)
                            T["red", n] = dve.do(lambda e, acc=acc, r2=r2: e.tensor_reduce(
                                UF[r2], acc.rearrange("p (j f) -> p f j", j=3), AX_X, ALU.add), T["mm", n], get(("split", n - 2)))
                            if k:
                                T["u", n] = dve.chain(lambda e, r=r, r2=r2, db=db: e.scalar_tensor_tensor(UF[r2], UF[r2], dinv2[:, db:db + 1], TX[r], ALU.mult, ALU.add), T["tx", n])
                            else:
                                T["u", n] = T["split", n] = dve.chain(lambda e, r=r, r2=r2, db=db: e.scalar_tensor_tensor(
                                    Y[:, db, :], UF[r2], dinv[:, db:db + 1], TX[r], ALU.mult, ALU.add), T["tx", n])
                        else:
                            T["u", n] = dve.do(lambda e, r=r, r2=r2: e.tensor_copy(UF[r2], TX[r]), T["tx", n], get(("split", n - 2)))
                        if k:
                            part = [new[:, db, j * D:(j + 1) * D] for j in range(3)]
                            T["hi", n] = act.do(lambda e, r2=r2, part=part: e.activation(part[0], UF[r2], ACT.Copy), T["u", n], get(("mm", n - db - 1)))
                            dve.do(lambda e, r2=r2, part=part: e.tensor_tensor(R1[r2], UF[r2], part[0], ALU.subtract), T["hi", n])
                            dve.chain(lambda e, r2=r2, part=part: e.tensor_copy(part[1], R1[r2]))
                            T["split", n] = dve.chain(lambda e, r2=r2, part=part: e.tensor_tensor(part[2], R1[r2], part[1], ALU.subtract))
                        n += 1

            if diffusion is None:
                windows()
            else:
                diffusion(TB, Y)
            barrier()
            space = Space(tables_at + NB * 3 * D)
            Wi, Wr, Bi = (space.get([D]) for _ in range(3))
            Xr = [space.get([4, D]) for _ in range(2)]
            YT = [at(tables_at + NB * 3 * D // 2 + k * 4 * D, [4 * D]) for k in range(2)]
            XO = [at(tables_at + NB * 3 * D // 2 + (2 + k) * 4 * D, [4, D]) for k in range(2)]
            ld2.dma(sp, lambda e: e.dma_start(Wi, a["L3_gnn_init_weight"][0]))
            ld2.dma(sp, lambda e: e.dma_start(Wr, a["L3_gnn_root_weight"][0, 0]))
            w = load_row(ld2, Bi, a["L3_gnn_bias"][0, 0, 0])
            xl = [landing(f"xl{k}") for k in range(2)]
            ol = [landing(f"ol{k}") for k in range(2)]
            for g, (b0, n) in enumerate(groups()):
                k = g % 2
                T["x", g] = xl[k].dma(sp, lambda e, k=k, b0=b0, n=n: e.dma_start(Xr[k][:, 0:n, :], blocks(x_rows)[:, b0:b0 + n, :]), get(("o", g - 2)))
                for q in range(n):
                    m = pe.do(lambda e, q=q, k=k, b0=b0: e.transpose(banks[:, k, q * P:(q + 1) * P], Y[:, b0 + q, :], ident), get(("yt", g - 2)))
                T["yt", g] = act.do(lambda e, k=k, n=n: e.activation(YT[k][:, 0:n * P], banks[:, k, 0:n * P], ACT.Copy), m, get(("mo", g - 2)))
                for q in range(n):
                    ov = banks[:, 2 + k, q * D:(q + 1) * D]
                    pe.quiet(lambda e, q=q, k=k, ov=ov: e.matmul(ov, YT[k][:, q * P:(q + 1) * P], Wi, start=True, stop=False), T["yt", g], w, get(("b", g - 2)))
                    T["mo", g] = pe.do(lambda e, q=q, k=k, ov=ov: e.matmul(ov, YT[k][:, q * P:(q + 1) * P], Wr, start=False, stop=True))
                xo = XO[k][:, 0:n, :]
                T["b", g] = dve.do(lambda e, k=k, n=n, xo=xo: e.tensor_tensor(
                    xo, banks[:, 2 + k, 0:n * D].rearrange("p (b f) -> p b f", f=D), Bi.unsqueeze(1).broadcast_to([P, n, D]), ALU.add), T["mo", g], w, get(("s", g - 2)))
                T["o", g] = dve.chain(lambda e, k=k, n=n, xo=xo: e.scalar_tensor_tensor(xo, xo, 0.0, Xr[k][:, 0:n, :], ALU.max, ALU.add), T["x", g])
                if b0 + n < NB:
                    T["s", g] = ol[k].dma(act, lambda e, b0=b0, n=n, xo=xo: e.dma_start(blocks(out[b0 * P:(b0 + n) * P, :]), xo), T["o", g])
                else:
                    r = N - b0 * P
                    T["s", g] = ol[k].dma(act, lambda e, b0=b0, r=r, xo=xo: e.dma_start(out[b0 * P:N, :], xo[0:r, 0, :]), T["o", g])


        low = Space(ring_at + 2 * NP, CW)
        KI, GI, DI = (low.get([1], I32) for _ in range(3))
        WV, KF, DUMP, CNT, MARK = (low.get([1]) for _ in range(5))
        EQ, TRI, PR = (low.get([P]) for _ in range(3))
        GR = low.get([2 * D + H])
        EDG, ZG, MG = (low.get([H]) for _ in range(3))
        COLS = (H + 1) * D + H + 1
        V, CUR = low.get([COLS]), low.get([COLS])
        t_sum = [dram(f"any_sums{i}", [NP + P, D + 1]) for i in range(2)]
        t_att = [dram(f"any_attention{i}", [NP + P, COLS]) for i in range(2)]
        t_max = [dram(f"any_maxima{i}", [NP + P, H]) for i in range(2)]
        t_dif = dram("any_diffusion", [NP + P, D])
        t_src = dram("any_sources", [NP, D])

        def serial(fill):
            barrier()
            s = Serial(turn_sems, pool_landed)
            s.step(dve, lambda e, i: e.memset(MARK, 0.0))
            fill(s)
            s.step(dve, lambda e, i: e.memset(MARK, 0.0))
            s.close(dve)
            dve.do(lambda e: e.memset(MARK, 0.0))
            barrier()

        def setup_any(s):
            s.step(pool, lambda e, i: e.memset(TRI, 1.0))
            s.step(pool, lambda e, i: e.affine_select(out=TRI, in_=TRI, compare_op=ALU.is_ge, fill=0.0, base=-1,
                                                      pattern=[[-1, P]], channel_multiplier=1))
            s.step(pool, lambda e, i: e.iota(DI, [[0, 1]], base=NP, channel_multiplier=1))
            s.step(dve, lambda e, i: e.tensor_copy(DUMP, DI))

        def fill_table(s, table, value, cols):
            n = table.shape[0] // P
            s.step(dve, lambda e, i: e.memset(V[:, 0:cols], value))
            s.step(sp, lambda e, i: e.dma_start(table.rearrange("(b p) f -> p b f", p=P), V[:, 0:cols].unsqueeze(1).broadcast_to([P, n, cols])))

        def scatter(s, table, cols, key, other, values, biggest=False):
            def rows(dst, src, index):
                return lambda e, i: e.indirect_dma_start(dst, None, src, bass.IndirectOffsetOnAxis(ap=index.bitcast(U32), axis=0))

            def fill():
                part = lambda v, i: v[0:1, bass.ds(i * P + 1, P)].rearrange("o p -> p o")
                s.step(dve, lambda e, i: e.memset(MARK, 0.0))
                s.step(sp, lambda e, i: e.dma_start(KI, part(key, i)))
                s.step(sp, lambda e, i: e.dma_start(GI, part(other, i)))
                s.step(sp, lambda e, i: e.dma_start(WV, part(weight_flat, i)))
                s.step(dve, lambda e, i: e.tensor_copy(KF, KI))
                s.step(pe, lambda e, i: e.matmul(banks[:, 0, 0:P], KF.broadcast_to([P, P]), ident, start=True, stop=True))
                s.step(dve, lambda e, i: e.tensor_scalar(EQ, banks[:, 0, 0:P], KF, None, ALU.is_equal))
                s.step(dve, lambda e, i: e.tensor_tensor(PR, EQ, TRI, ALU.mult))
                s.step(dve, lambda e, i: e.tensor_reduce(CNT, PR, AX_X, ALU.add))
                s.step(dve, lambda e, i: e.tensor_scalar(CNT, CNT, 0.0, None, ALU.is_equal))
                s.step(dve, lambda e, i: e.tensor_tensor(KF, KF, DUMP, ALU.subtract))
                s.step(dve, lambda e, i: e.tensor_tensor(KF, KF, CNT, ALU.mult))
                s.step(dve, lambda e, i: e.tensor_tensor(KF, KF, DUMP, ALU.add))
                s.step(dve, lambda e, i: e.tensor_copy(DI, KF))
                values(rows)
                s.pool_dma(pool, rows(CUR[:, 0:cols], table, KI))
                if biggest:
                    s.step(dve, lambda e, i: e.tensor_scalar(EQ, EQ, -1.0, BIG, ALU.add, ALU.mult))
                    for h in range(cols):
                        s.step(pe, lambda e, i, h=h: e.matmul(banks[:, 1, 0:P], V[:, h:h + 1].broadcast_to([P, P]), ident, start=True, stop=True))
                        s.step(dve, lambda e, i: e.tensor_tensor(PR, banks[:, 1, 0:P], EQ, ALU.add))
                        s.step(dve, lambda e, i: e.tensor_reduce(CNT, PR, AX_X, ALU.max))
                        s.step(dve, lambda e, i, h=h: e.tensor_tensor(CUR[:, h:h + 1], CUR[:, h:h + 1], CNT, ALU.max))
                else:
                    for b, c in enumerate(range(0, cols, 512)):
                        n = min(512, cols - c)
                        s.step(pe, lambda e, i, b=b, c=c, n=n: e.matmul(banks[:, 1 + b, 0:n], EQ, V[:, c:c + n], start=True, stop=True))
                        s.step(dve, lambda e, i, b=b, c=c, n=n: e.tensor_tensor(CUR[:, c:c + n], CUR[:, c:c + n], banks[:, 1 + b, 0:n], ALU.add))
                s.pool_dma(pool, lambda e, i: e.indirect_dma_start(table, bass.IndirectOffsetOnAxis(ap=DI.bitcast(U32), axis=0), CUR[:, 0:cols], None))
            s.loop(NC, fill)

        def any_sums(layer):
            key, other, rows_in, into = ((dst_flat, src_flat, h_table, ACC0), (src_flat, dst_flat, h_rows, AGG))[layer]
            LB = at(0, [D + 1])

            def go(s):
                if layer == 0:
                    setup_any(s)
                fill_table(s, t_sum[layer], 0.0, D + 1)

                def values(rows):
                    s.pool_dma(pool, rows(GR[:, 0:D], rows_in, GI))
                    if layer == 0:
                        s.step(dve, lambda e, i: e.tensor_scalar(V[:, 0:D], GR[:, 0:D], WV, None, ALU.mult))
                    else:
                        s.step(dve, lambda e, i: e.tensor_copy(V[:, 0:D], GR[:, 0:D]))
                    s.step(dve, lambda e, i: e.memset(V[:, D:D + 1], 1.0))

                scatter(s, t_sum[layer], D + 1, key, other, values)
                s.step(dve, lambda e, i: e.memset(MARK, 0.0))
                for b in range(NB):
                    s.step(sp, lambda e, i, b=b: e.dma_start(LB, t_sum[layer][b * P:(b + 1) * P, :]))
                    s.step(pe, lambda e, i: e.transpose(banks[:, 0, 0:P], LB[:, 0:D], ident))
                    s.step(dve, lambda e, i, b=b: e.tensor_copy(into[:, b * P:(b + 1) * P], banks[:, 0, 0:P]))
                    if layer:
                        s.step(dve, lambda e, i, b=b: e.tensor_copy(odeg[:, b:b + 1], LB[:, D:D + 1]))
            serial(go)

        def any_attention(i2):
            table, row = (gat0_table, D + H) if i2 == 0 else (gat1_table, 2 * D + H)
            LB = at(ring_at, [COLS])

            def go(s):
                fill_table(s, t_max[i2], -BIG, H)
                fill_table(s, t_att[i2], 0.0, COLS)

                def logits(rows, out):
                    s.pool_dma(pool, rows(GR[:, 0:row], table, GI))
                    s.pool_dma(pool, rows(EDG, ed_table[i2], KI))
                    s.step(dve, lambda e, i: e.tensor_tensor(ZG, GR[:, D:D + H], EDG, ALU.add))
                    s.step(dve, lambda e, i: e.scalar_tensor_tensor(out, ZG, 0.2, ZG, ALU.mult, ALU.max))

                scatter(s, t_max[i2], H, dst_flat, src_flat, lambda rows: logits(rows, V[:, 0:H]), biggest=True)

                def values(rows):
                    logits(rows, EDG)
                    s.pool_dma(pool, rows(MG, t_max[i2], KI))
                    s.step(dve, lambda e, i: e.tensor_tensor(ZG, EDG, MG, ALU.subtract))
                    s.step(act, lambda e, i: e.activation(ZG, ZG, ACT.Exp))
                    s.step(dve, lambda e, i: e.tensor_tensor(
                        V[:, 0:H * D].rearrange("p (h f) -> p h f", f=D), GR[:, 0:D].unsqueeze(1).broadcast_to([P, H, D]),
                        ZG.unsqueeze(2).broadcast_to([P, H, D]), ALU.mult))
                    second = GR[:, 0:D] if i2 == 0 else GR[:, D + H:]
                    s.step(dve, lambda e, i: e.tensor_scalar(V[:, H * D:(H + 1) * D], second, WV, None, ALU.mult))
                    s.step(dve, lambda e, i: e.tensor_copy(V[:, (H + 1) * D:COLS - 1], ZG))
                    s.step(dve, lambda e, i: e.tensor_copy(V[:, COLS - 1:COLS], WV))

                scatter(s, t_att[i2], COLS, dst_flat, src_flat, values)
                s.step(dve, lambda e, i: e.memset(MARK, 0.0))
                for b in range(NB):
                    s.step(sp, lambda e, i, b=b: e.dma_start(LB, t_att[i2][b * P:(b + 1) * P, :]))
                    for h in range(H + 1):
                        s.step(pe, lambda e, i, h=h: e.transpose(banks[:, 0, 0:P], LB[:, h * D:(h + 1) * D], ident))
                        s.step(dve, lambda e, i, b=b, h=h: e.tensor_copy(ACC[:, h, b * P:(b + 1) * P], banks[:, 0, 0:P]))
                    s.step(pe, lambda e, i: e.transpose(banks[0:H + 1, 0, 0:P], LB[:, (H + 1) * D:COLS], ident))
                    s.step(dve, lambda e, i, b=b: e.tensor_copy(SACC[:, b * P:(b + 1) * P], banks[0:H + 1, 0, 0:P]))
            serial(go)

        def any_diffusion(TB, Y):
            space = Space(0, ring_at)
            HX, U, DG = space.get([NB, D]), space.get([NB, D]), space.get([NB])

            def go(s):
                s.step(sp, lambda e, i: e.dma_start(HX, blocks(h_rows)))
                s.step(sp, lambda e, i: e.dma_start(DG.unsqueeze(2), blocks(t_sum[0][0:NP, :])[:, :, D:D + 1]))
                s.step(dve, lambda e, i: e.tensor_scalar_add(DG, DG, 1.0))
                s.step(act, lambda e, i: e.activation(DG, DG, ACT.Sqrt))
                s.step(dve, lambda e, i: e.reciprocal(DG, DG))
                by_degree = DG.unsqueeze(2).broadcast_to([P, NB, D])
                s.step(dve, lambda e, i: e.tensor_tensor(Y, HX, TB[:, STEPS - 1, :].unsqueeze(1).broadcast_to([P, NB, D]), ALU.mult))
                for k in range(STEPS - 2, -1, -1):
                    s.step(dve, lambda e, i: e.tensor_tensor(U, Y, by_degree, ALU.mult))
                    s.step(sp, lambda e, i: e.dma_start(blocks(t_src), U))
                    s.step(sp, lambda e, i: e.dma_start(blocks(t_dif[0:NP, :]), U))
                    s.step(sp, lambda e, i: e.dma_start(t_dif[NP:NP + P, :], U[:, 0, :]))
                    scatter(s, t_dif, D, dst_flat, src_flat, lambda rows: s.pool_dma(pool, rows(V[:, 0:D], t_src, GI)))
                    s.step(dve, lambda e, i: e.memset(MARK, 0.0))
                    s.step(sp, lambda e, i: e.dma_start(U, blocks(t_dif[0:NP, :])))
                    s.step(dve, lambda e, i: e.tensor_tensor(U, U, by_degree, ALU.mult))
                    s.step(dve, lambda e, i, k=k: e.tensor_tensor(Y, HX, TB[:, k, :].unsqueeze(1).broadcast_to([P, NB, D]), ALU.mult))
                    s.step(dve, lambda e, i: e.tensor_tensor(Y, Y, U, ALU.add))
            serial(go)

        def regular():
            layer0_edges()
            layer0_nodes()
            layer1_sums()
            layer1_nodes()
            layer2_tables0()
            layer2_edges(0)
            layer2_nodes0()
            layer2_edges(1)
            layer2_nodes1()
            layer3(None)
            barrier()

        def any_edges():
            any_sums(0)
            layer0_nodes()
            any_sums(1)
            layer1_nodes()
            layer2_tables0()
            any_attention(0)
            layer2_nodes0()
            any_attention(1)
            layer2_nodes1()
            layer3(any_diffusion)
            barrier()

        counts, landed = snapshot()
        take(common)
        for name, program in (("regular", regular), ("any", any_edges)):
            for l in lanes:
                l.count, l.waited = counts[id(l)][0], dict(counts[id(l)][1])
            for x in landings:
                x.count = landed.get(id(x), 0)
            program()
            branches[name] = {}
            take(branches[name])
        finish()


_OUTS = [((N, D), "float32")]


def kernel(**inputs):
    import numpy as _np
    import concourse.bacc as _bacc
    from concourse import mybir as _mybir
    from concourse.bass_utils import run_bass_kernel_spmd as _run

    nc = _bacc.Bacc("TRN2", target_bir_lowering=False, num_devices=1)
    arrays, args = {}, {}
    for name in inputs:
        v = _np.ascontiguousarray(inputs[name])
        arrays[f"in_{name}"] = v
        args[name] = nc.dram_tensor(f"in_{name}", v.shape, _mybir.dt.from_np(v.dtype), kind="ExternalInput").ap()
    out = nc.dram_tensor("out", [N, D], F32, kind="ExternalOutput").ap()
    build(nc, args, out)
    r = _run(nc, [arrays], core_ids=[0])
    return r.results[0]["out"]
```
